# Optimizing a Trainium2 kernel written in Bass

```python
import numpy as np
import jax
import jax.numpy as jnp

def _softmax(x, axis=-1):
    return jax.nn.softmax(x, axis=axis)

def _gelu(x):
    return jax.nn.gelu(x, approximate=True)

def _silu(x):
    return jax.nn.silu(x)

def _sigmoid(x):
    return jax.nn.sigmoid(x)

def _layernorm(x, axis=-1, eps=1e-05):
    m = jnp.mean(x, axis=axis, keepdims=True)
    v = jnp.var(x, axis=axis, keepdims=True)
    return (x - m) / jnp.sqrt(v + eps)

def _scatter_add(tgt, idx, src, axis=0):
    return tgt.at[idx].add(src)

def _segment_sum(src, seg, n):
    return jax.ops.segment_sum(src, seg, n)
kernel_name = 'mk_seq_postln_d2_jaxref_r8_908736'

def setup_inputs(seed: int=0):
    np.random.seed(seed)
    _w = jnp.asarray

    def _L0_attn_setup():
        import jax, jax.numpy as jnp
        import numpy as np
        NEG_INF = -1e+30

        def rotary_pos_emb(x):
            B, T, H, D = x.shape
            exponents = (jnp.arange(0, D, 2)[:D // 2] // D).astype(jnp.float32)
            freqs = 1.0 / jnp.power(jnp.float32(1000.0), exponents)
            theta = jnp.arange(T, dtype=jnp.float32)[:, None] * freqs[None, :]
            cos = jnp.cos(theta)[None, :, None, :]
            sin = jnp.sin(theta)[None, :, None, :]
            xr = x.astype(jnp.float32).reshape(B, T, H, D // 2, 2)
            x0, x1 = (xr[..., 0], xr[..., 1])
            out = jnp.stack([x0 * cos - x1 * sin, x0 * sin + x1 * cos], axis=-1)
            return out.reshape(B, T, H, D).astype(x.dtype)

        def attention_fwd(x, wq, wk, wv, wo, n_heads=32):
            B, T, C = x.shape
            hd = C // n_heads
            xq = (x @ wq.T).reshape(B, T, n_heads, hd)
            xk = (x @ wk.T).reshape(B, T, n_heads, hd)
            xv = (x @ wv.T).reshape(B, T, n_heads, hd)
            xq = rotary_pos_emb(xq)
            xk = rotary_pos_emb(xk)
            scale = hd ** (-0.5)
            scores = jnp.einsum('bqhd,bkhd->bhqk', xq, xk) * scale
            causal = jnp.tril(jnp.ones((T, T), dtype=bool))
            scores = jnp.where(causal[None, None], scores, NEG_INF)
            probs = jax.nn.softmax(scores.astype(jnp.float32), axis=-1).astype(xq.dtype)
            out = jnp.einsum('bhqk,bkhd->bqhd', probs, xv).reshape(B, T, C)
            return out @ wo.T
        key = jax.random.key(seed)
        ks = jax.random.split(key, 5)
        B, T, C = (2, 256, 512)
        s = 0.02
        return {'x': jax.random.normal(ks[0], (B, T, C), jnp.float32), 'wq': jax.random.normal(ks[1], (C, C), jnp.float32) * s, 'wk': jax.random.normal(ks[2], (C, C), jnp.float32) * s, 'wv': jax.random.normal(ks[3], (C, C), jnp.float32) * s, 'wo': jax.random.normal(ks[4], (C, C), jnp.float32) * s}
    _L0_attn_in = _L0_attn_setup()

    def _L0_ffn_setup():
        import jax, jax.numpy as jnp
        import numpy as np
        HID, INTER = (512, 1792)
        B, S = (2, 256)

        def _binary_diff_weight(w, base):
            d = w - base
            coeff = jnp.mean(jnp.abs(d))
            return base + coeff * jnp.sign(d)
        key = jax.random.key(seed)
        ks = jax.random.split(key, 7)
        return {'hidden_states': jax.random.normal(ks[0], (B, S, HID), dtype=jnp.float32), 'w1': jax.random.normal(ks[1], (INTER, HID), dtype=jnp.float32) * 0.02, 'mean_w1': jax.random.normal(ks[2], (INTER, HID), dtype=jnp.float32) * 0.02, 'w2': jax.random.normal(ks[3], (HID, INTER), dtype=jnp.float32) * 0.02, 'mean_w2': jax.random.normal(ks[4], (HID, INTER), dtype=jnp.float32) * 0.02, 'w3': jax.random.normal(ks[5], (INTER, HID), dtype=jnp.float32) * 0.02, 'mean_w3': jax.random.normal(ks[6], (INTER, HID), dtype=jnp.float32) * 0.02}
    _L0_ffn_in = _L0_ffn_setup()

    def _L1_attn_setup():
        import math
        import jax, jax.numpy as jnp
        import numpy as np

        def _rope_tables(T, h, dtype):
            pos = jnp.arange(T, dtype=jnp.float32)
            thetas = 1.0 / 10000.0 ** (jnp.arange(0, h, 2, dtype=jnp.float32) / h)
            pt = jnp.outer(pos, thetas)
            pt = jnp.concatenate([pt, pt], axis=-1)
            return (jnp.sin(pt).astype(dtype), jnp.cos(pt).astype(dtype))

        def _apply_rope(x, sin, cos):
            h = x.shape[-1]
            rot = jnp.concatenate([-x[..., h // 2:], x[..., :h // 2]], axis=-1)
            return x * cos + rot * sin
        key = jax.random.key(seed)
        ks = jax.random.split(key, 5)
        B, T, C = (2, 256, 512)
        s = 1.0 / math.sqrt(C)
        return {'x': jax.random.normal(ks[0], (B, T, C), dtype=jnp.float32), 'wq': jax.random.normal(ks[1], (C, C), dtype=jnp.float32) * s, 'wk': jax.random.normal(ks[2], (C, C), dtype=jnp.float32) * s, 'wv': jax.random.normal(ks[3], (C, C), dtype=jnp.float32) * s, 'wo': jax.random.normal(ks[4], (C, C), dtype=jnp.float32) * s}
    _L1_attn_in = _L1_attn_setup()

    def _L1_ffn_setup():
        import jax, jax.numpy as jnp
        import numpy as np
        BLOCK = 64
        NF4_CODE = jnp.array([-1.0, -0.6961928009986877, -0.5250730514526367, -0.39491748809814453, -0.28444138169288635, -0.18477343022823334, -0.09105003625154495, 0.0, 0.07958029955625534, 0.16093020141124725, 0.24611230194568634, 0.33791524171829224, 0.44070982933044434, 0.5626170039176941, 0.7229568362236023, 1.0], dtype=jnp.float32)

        def dequantize_nf4(w_idx, absmax):
            out_f, in_f = w_idx.shape
            w = NF4_CODE[w_idx.reshape(-1, BLOCK)] * absmax[:, None]
            return w.reshape(out_f, in_f)
        key = jax.random.key(seed)
        k1, k2, k3, k4 = jax.random.split(key, 4)
        out_f, in_f = (512, 512)
        x = jax.random.normal(k1, (4, 256, in_f), dtype=jnp.float32)
        w_idx = jax.random.randint(k2, (out_f, in_f), 0, 16, dtype=jnp.int32)
        absmax = jax.random.uniform(k3, (out_f * in_f // BLOCK,), dtype=jnp.float32)
        bias = jax.random.normal(k4, (out_f,), dtype=jnp.float32)
        return {'x': x, 'w_idx': w_idx, 'absmax': absmax, 'bias': bias}
    _L1_ffn_in = _L1_ffn_setup()
    _d = {'L0_attn_x': _L0_attn_in['x'], 'L0_attn_wq': _L0_attn_in['wq'], 'L0_attn_wk': _L0_attn_in['wk'], 'L0_attn_wv': _L0_attn_in['wv'], 'L0_attn_wo': _L0_attn_in['wo'], 'L0_ffn_w1': _L0_ffn_in['w1'], 'L0_ffn_mean_w1': _L0_ffn_in['mean_w1'], 'L0_ffn_w2': _L0_ffn_in['w2'], 'L0_ffn_mean_w2': _L0_ffn_in['mean_w2'], 'L0_ffn_w3': _L0_ffn_in['w3'], 'L0_ffn_mean_w3': _L0_ffn_in['mean_w3'], 'L1_attn_wq': _L1_attn_in['wq'], 'L1_attn_wk': _L1_attn_in['wk'], 'L1_attn_wv': _L1_attn_in['wv'], 'L1_attn_wo': _L1_attn_in['wo'], 'L1_ffn_w_idx': _L1_ffn_in['w_idx'], 'L1_ffn_absmax': _L1_ffn_in['absmax'], 'L1_ffn_bias': _L1_ffn_in['bias']}
    _x0 = _d['L0_attn_x']
    _d['L0_attn_x'] = jax.random.normal(jax.random.fold_in(jax.random.key(seed), 1), (4, 512, 512), dtype=_x0.dtype)
    del _x0
    return _d

def reference(L0_attn_x, L0_attn_wq, L0_attn_wk, L0_attn_wv, L0_attn_wo, L0_ffn_w1, L0_ffn_mean_w1, L0_ffn_w2, L0_ffn_mean_w2, L0_ffn_w3, L0_ffn_mean_w3, L1_attn_wq, L1_attn_wk, L1_attn_wv, L1_attn_wo, L1_ffn_w_idx, L1_ffn_absmax, L1_ffn_bias):

    def _L0_attn_ref(x, wq, wk, wv, wo):
        import jax, jax.numpy as jnp
        import numpy as np
        NEG_INF = -1e+30

        def rotary_pos_emb(x):
            B, T, H, D = x.shape
            exponents = (jnp.arange(0, D, 2)[:D // 2] // D).astype(jnp.float32)
            freqs = 1.0 / jnp.power(jnp.float32(1000.0), exponents)
            theta = jnp.arange(T, dtype=jnp.float32)[:, None] * freqs[None, :]
            cos = jnp.cos(theta)[None, :, None, :]
            sin = jnp.sin(theta)[None, :, None, :]
            xr = x.astype(jnp.float32).reshape(B, T, H, D // 2, 2)
            x0, x1 = (xr[..., 0], xr[..., 1])
            out = jnp.stack([x0 * cos - x1 * sin, x0 * sin + x1 * cos], axis=-1)
            return out.reshape(B, T, H, D).astype(x.dtype)

        def attention_fwd(x, wq, wk, wv, wo, n_heads=32):
            B, T, C = x.shape
            hd = C // n_heads
            xq = (x @ wq.T).reshape(B, T, n_heads, hd)
            xk = (x @ wk.T).reshape(B, T, n_heads, hd)
            xv = (x @ wv.T).reshape(B, T, n_heads, hd)
            xq = rotary_pos_emb(xq)
            xk = rotary_pos_emb(xk)
            scale = hd ** (-0.5)
            scores = jnp.einsum('bqhd,bkhd->bhqk', xq, xk) * scale
            causal = jnp.tril(jnp.ones((T, T), dtype=bool))
            scores = jnp.where(causal[None, None], scores, NEG_INF)
            probs = jax.nn.softmax(scores.astype(jnp.float32), axis=-1).astype(xq.dtype)
            out = jnp.einsum('bhqk,bkhd->bqhd', probs, xv).reshape(B, T, C)
            return out @ wo.T
        return attention_fwd(x, wq, wk, wv, wo)

    def _L0_ffn_ref(hidden_states, w1, mean_w1, w2, mean_w2, w3, mean_w3):
        import jax, jax.numpy as jnp
        import numpy as np
        HID, INTER = (512, 1792)
        B, S = (2, 256)

        def _binary_diff_weight(w, base):
            d = w - base
            coeff = jnp.mean(jnp.abs(d))
            return base + coeff * jnp.sign(d)
        W1 = _binary_diff_weight(w1, mean_w1)
        W2 = _binary_diff_weight(w2, mean_w2)
        W3 = _binary_diff_weight(w3, mean_w3)
        gate = jnp.einsum('bsh,ih->bsi', hidden_states, W1)
        up = jnp.einsum('bsh,ih->bsi', hidden_states, W3)
        h = jax.nn.silu(gate) * up
        return jnp.einsum('bsi,hi->bsh', h, W2)

    def _L1_attn_ref(x, wq, wk, wv, wo):
        import math
        import jax, jax.numpy as jnp
        import numpy as np

        def _rope_tables(T, h, dtype):
            pos = jnp.arange(T, dtype=jnp.float32)
            thetas = 1.0 / 10000.0 ** (jnp.arange(0, h, 2, dtype=jnp.float32) / h)
            pt = jnp.outer(pos, thetas)
            pt = jnp.concatenate([pt, pt], axis=-1)
            return (jnp.sin(pt).astype(dtype), jnp.cos(pt).astype(dtype))

        def _apply_rope(x, sin, cos):
            h = x.shape[-1]
            rot = jnp.concatenate([-x[..., h // 2:], x[..., :h // 2]], axis=-1)
            return x * cos + rot * sin
        B, T, C = x.shape
        n_head = 32
        h = C // n_head

        def proj(w):
            y = jnp.einsum('btc,dc->btd', x, w)
            return y.reshape(B, T, n_head, h).transpose(0, 2, 1, 3)
        q, k, v = (proj(wq), proj(wk), proj(wv))
        sin, cos = _rope_tables(T, h, x.dtype)
        q = _apply_rope(q, sin, cos)
        k = _apply_rope(k, sin, cos)
        scores = jnp.einsum('bnth,bnsh->bnts', q, k) * (1.0 / math.sqrt(h))
        causal = jnp.tril(jnp.ones((T, T), dtype=bool))
        scores = jnp.where(causal, scores, -jnp.inf)
        attn = jax.nn.softmax(scores, axis=-1)
        out = jnp.einsum('bnts,bnsh->bnth', attn, v)
        out = out.transpose(0, 2, 1, 3).reshape(B, T, C)
        return jnp.einsum('btc,dc->btd', out, wo)

    def _L1_ffn_ref(x, w_idx, absmax, bias):
        import jax, jax.numpy as jnp
        import numpy as np
        BLOCK = 64
        NF4_CODE = jnp.array([-1.0, -0.6961928009986877, -0.5250730514526367, -0.39491748809814453, -0.28444138169288635, -0.18477343022823334, -0.09105003625154495, 0.0, 0.07958029955625534, 0.16093020141124725, 0.24611230194568634, 0.33791524171829224, 0.44070982933044434, 0.5626170039176941, 0.7229568362236023, 1.0], dtype=jnp.float32)

        def dequantize_nf4(w_idx, absmax):
            out_f, in_f = w_idx.shape
            w = NF4_CODE[w_idx.reshape(-1, BLOCK)] * absmax[:, None]
            return w.reshape(out_f, in_f)
        w = dequantize_nf4(w_idx, absmax)
        return jnp.einsum('bsi,oi->bso', x, w) + bias
    x = L0_attn_x
    x = _layernorm(x + _L0_attn_ref(x, L0_attn_wq, L0_attn_wk, L0_attn_wv, L0_attn_wo), axis=-1)
    x = _layernorm(x + _L0_ffn_ref(x, L0_ffn_w1, L0_ffn_mean_w1, L0_ffn_w2, L0_ffn_mean_w2, L0_ffn_w3, L0_ffn_mean_w3), axis=-1)
    x = _layernorm(x + _L1_attn_ref(x, L1_attn_wq, L1_attn_wk, L1_attn_wv, L1_attn_wo), axis=-1)
    x = _layernorm(x + _L1_ffn_ref(x, L1_ffn_w_idx, L1_ffn_absmax, L1_ffn_bias), axis=-1)
    return x

_drawn_inputs = setup_inputs


def setup_inputs(seed=0):
    import zlib

    import numpy as np

    out = dict(_drawn_inputs(seed))
    spreads = {}
    factors = {'L0_attn_wq': 8.0, 'L0_attn_wk': 8.0}
    for name, (base, spread) in spreads.items():
        noise = np.random.default_rng([zlib.crc32(name.encode()), seed]).standard_normal(out[name].shape)
        drawn = base * np.exp(spread * noise) if base else spread * noise
        out[name] = jnp.asarray(drawn.astype(out[name].dtype))
    for name, factor in factors.items():
        out[name] = (out[name] * factor).astype(out[name].dtype)
    return out
```

```python
from contextlib import ExitStack

import numpy as np

import concourse.bass as bass
from concourse import mybir

ALU = mybir.AluOpType
ACT = mybir.ActivationFunctionType
AX = mybir.AxisListType
F32 = mybir.dt.float32
F32R = mybir.dt.float32r
BF16 = mybir.dt.bfloat16
I32 = mybir.dt.int32

P = 128
B, T, C = 4, 512, 512
H = 32
D = C // H
KT = C // P
TT = T // P
F = 1792
FT = F // P
NB = 512
QUAD = 4
NQ = H // QUAD
RING = 4
PTR = 6
LAG = 2
NSLOT = 6
ROWS = NSLOT * D
SC = T + 384 + 256 + 128
S_AT = {3: 0, 2: 512, 0: 896, 1: 1024}
ST_AT = {0: 0, 3: 512, 1: 640, 2: 1024}
EPS = 1e-5
NF4 = [-1.0, -0.6961928009986877, -0.5250730514526367, -0.39491748809814453, -0.28444138169288635,
       -0.18477343022823334, -0.09105003625154495, 0.0, 0.07958029955625534, 0.16093020141124725,
       0.24611230194568634, 0.33791524171829224, 0.44070982933044434, 0.5626170039176941,
       0.7229568362236023, 1.0]



class Steps:

    def __init__(self, eng, sem, base, per):
        self.eng, self.sem, self.base, self.per, self.n = eng, sem, base, per, 0

    def inc(self, ins):
        ins.then_inc(self.sem, 1)
        self.n += 1

    def wait(self):
        self.eng.wait_ge(self.sem, self.base + self.n)

    def done(self, ins):
        self.inc(ins)
        self.wait()

    def end(self):
        assert self.n == self.per, (self.n, self.per)


def product3(eng, out, lhs, rhs, start=True, stop=True):
    (lh, ll), (rh, rl) = lhs, rhs
    eng.matmul(out, lh, rh, start=start, stop=False)
    eng.matmul(out, lh, rl, start=False, stop=False)
    return eng.matmul(out, ll, rh, start=False, stop=stop)


NORM_STEPS = 2 * TT + 5


def norm_rows(dve, st, y, stats, mv, small, root_asked, rooted, normed, b):
    for t in range(TT):
        st.inc(dve.bn_stats(stats[:, t, :], y[:, t, :]))
    st.wait()
    dve.memset(small[:, 2, :], 0.0)
    for t in range(TT):
        st.inc(dve.bn_aggr(mv[:, t, :], stats[:, t, :]))
    st.wait()
    dve.tensor_scalar(small[:, 0, :], mv[:, :, 1], EPS, None, ALU.add).then_inc(root_asked, 1)
    dve.wait_ge(rooted, b + 1)
    dve.wait_ge(root_asked, b + 1)
    v, s, r = small[:, 0, :], small[:, 1, :], small[:, 2, :]
    st.done(dve.reciprocal(r, s))
    st.done(dve.tensor_tensor(r, r, v, ALU.mult))
    st.done(dve.tensor_tensor(r, r, s, ALU.add))
    st.done(dve.tensor_scalar(r, r, 0.5, None, ALU.mult))
    st.done(dve.reciprocal(small[:, 3, :], r))
    for t in range(TT):
        dve.tensor_scalar(y[:, t, :], y[:, t, :], mv[:, t, 0:1], small[:, 3, t:t + 1],
                          ALU.subtract, ALU.mult).then_inc(normed, 1)


def flat(ap):
    return ap[:, :, :].rearrange("p a b -> p (a b)")


def attention_phase(nc, tag, x_in, xt_in, wts, cos_in, sin_in, ident_in, mask_in, x_out, xt_out,
                    q_planes, k_planes):
    with ExitStack() as ctx:
        def sb(name, shape, dt=F32, at=ctx):
            return at.enter_context(nc.sbuf_tensor(f"{tag}_{name}", shape, dt))

        def sem(name):
            return ctx.enter_context(nc.semaphore(f"{tag}_{name}"))

        w_hi = [sb(f"w{n}_hi", [P, KT, C], F32R) for n in "qkvo"]
        w_lo = [sb(f"w{n}_lo", [P, KT, C], F32R) for n in "qkvo"]
        xraw = sb("xraw", [P, KT, T])
        x_hi = sb("x_hi", [P, KT, T], F32R)
        x_lo = sb("x_lo", [P, KT, T], F32R)
        vaug = sb("vaug", [P, TT, H, D + 1])
        cosr = sb("cosr", [P, T])
        sinr = sb("sinr", [P, T])
        qs = sb("qs", [P, RING, QUAD * T], BF16)
        ks = sb("ks", [P, RING, QUAD * T], BF16)
        at_hi = sb("at_hi", [P, NQ // 2, T], F32R)
        at_lo = sb("at_lo", [P, NQ // 2, T], F32R)
        y = sb("y", [P, TT, T])
        planes = sb("planes", [P, 2, 3, T], BF16)
        u = sb("u", [P, 2, 16, 32])
        un = sb("un", [P, 16, 32])
        at = sb("at", [P, T])
        rec = sb("rec", [P, 16])
        xtile = sb("xtile", [P, 2, KT, P])
        ident = sb("ident", [P, P])
        identb = sb("identb", [P, P], BF16)
        masks = sb("masks", [P, 2, 2 * P], BF16)
        bmax = sb("bmax", [P, QUAD, 10])
        qmax = sb("qmax", [P, QUAD, TT])
        mplane = sb("mplane", [QUAD * TT, 3, P], BF16)
        mrest = xtile[0:QUAD * TT, 0, 0, :]
        stats = sb("stats", [P, TT, 6])
        mv = sb("mv", [P, TT, 2])
        small = sb("small", [P, 4, TT])
        with ExitStack() as early:
            wraw = sb("wraw", [P, 2, KT * C], at=early)
            maskraw = sb("maskraw", [P, 4 * P], at=early)
        pt = sb("pt", [P, PTR, SC])

        ps = [ctx.enter_context(nc.psum_tensor(f"{tag}_ps{i}", [P, 3 * NB], F32)) for i in range(2)]
        pv = ctx.enter_context(nc.psum_tensor(f"{tag}_pv", [P, 2 * NB], F32))

        def bank(n):
            return ps[n // 3][:, (n % 3) * NB:(n % 3 + 1) * NB]

        maxt = ps[0][0:QUAD * TT, SC:SC + P]

        w_loaded = [sem("w_loaded0"), sem("w_loaded1")]
        w_hi_done, w_done = sem("w_hi_done"), sem("w_done")
        const_in, consts, ones_set = sem("const_in"), sem("consts"), sem("ones_set")
        x_loaded, x_hi_done, x_done = sem("x_loaded"), sem("x_hi_done"), sem("x_done")
        proj_done, rope_read, v_copied = sem("proj_done"), sem("rope_read"), sem("v_copied")
        rope_sum, plane_h, rest_h, plane_m, plane_l = (
            sem("rope_sum"), sem("plane_h"), sem("rest_h"), sem("plane_m"), sem("plane_l"))
        plane_out = [sem("plane_out0"), sem("plane_out1")]
        stack_in = [sem(f"stack_in{r}") for r in range(RING)]
        s_done, s_read, qmax_done, maxt_done = sem("s_done"), sem("s_read"), sem("qmax_done"), sem("maxt_done")
        maxt_read, max_split = sem("maxt_read"), sem("max_split")
        max_in = [sem("max_in0"), sem("max_in1")]
        st_done, exp_done, pv_done, pv_read = sem("st_done"), sem("exp_done"), sem("pv_done"), sem("pv_read")
        at_ready, at_hi_done, at_lo_done = sem("at_ready"), sem("at_hi_done"), sem("at_lo_done")
        res_in, o_done, o_read = sem("res_in"), sem("o_done"), sem("o_read")
        root_asked, rooted, normed = sem("root_asked"), sem("rooted"), sem("normed")
        tr_done, tr_copied, x_stored = sem("tr_done"), sem("tr_copied"), sem("x_stored")
        xt_stored = [sem("xt_stored0"), sem("xt_stored1")]
        dve_steps = sem("dve_steps")
        DVE_PER = NQ * 3 + NQ * 3 + NQ * 2 + NORM_STEPS

        block = ctx.enter_context(nc.Block())

        q_runs = [(0, 3, 0, True), (3, 2, 1, True), (5, 1, 2, True)]
        k_runs = [(0, 3, 0, False), (3, 2, 0, False), (5, 1, 0, False)]
        LOADS = 9

        def load_stack(eng, b, q):
            for runs, dst, src in ((q_runs, qs, q_planes), (k_runs, ks, k_planes)):
                v = src[b, q // 2].rearrange("c (d h) t -> (c d) (h t)", h=2 * QUAD)
                cols = slice(q % 2 * QUAD * T, (q % 2 + 1) * QUAD * T)
                for slot, n, plane, same in runs:
                    k = 1 if same else n
                    for i in range(n // k):
                        eng.dma_start(dst[(slot + i) * D:(slot + i + k) * D, q % RING, :],
                                      v[plane * D:(plane + k) * D, cols]).then_inc(stack_in[q % RING], 16)

        @block.sync
        def _(sp):
            for n in range(4):
                if n >= 2:
                    sp.wait_ge(w_done, n - 1)
                sp.dma_start(wraw[:, n % 2, :], wts[n].rearrange("p k c -> p (k c)")).then_inc(w_loaded[n % 2], 16)
                if n == 0:
                    sp.dma_start(xraw[:, :, :], xt_in[0]).then_inc(x_loaded, 16)
                    sp.dma_start(cosr[:, :], cos_in).then_inc(const_in, 16)
                    sp.dma_start(sinr[:, :], sin_in).then_inc(const_in, 16)
                    sp.dma_start(ident[:, :], ident_in).then_inc(const_in, 16)
                    sp.dma_start(maskraw[:, :], mask_in).then_inc(const_in, 16)

            def body(b, more):
                if more:
                    sp.wait_ge(x_done, b + 1)
                    sp.dma_start(xraw[:, :, :], xt_in[b + 1]).then_inc(x_loaded, 16)
                sp.wait_ge(plane_out[0], 64 * b + 64)
                sp.wait_ge(plane_out[1], 64 * b + 64)
                sp.wait_ge(plane_l, 8 * b + 8)
                sp.dma_start(y[:, :, :], x_in[b].rearrange("(t p) c -> p t c", p=P)).then_inc(res_in, 16)

                def load(q):
                    if q >= RING:
                        sp.wait_ge(st_done, H * b + QUAD * (q - RING + 1))
                    else:
                        sp.wait_ge(st_done, H * b)
                    load_stack(sp, b, q)

                def maxima(q):
                    sp.wait_ge(max_split, NQ * b + q + 1)
                    for i in range(3):
                        sp.dma_start(qs[ROWS + i:ROWS + i + 1, q % RING, :].rearrange("p (m t) -> p m t", t=P),
                                     mplane[:, i, :]).then_inc(max_in[q % 2], 16)

                for q in range(RING):
                    load(q)
                maxima(0)
                maxima(1)
                for q in range(RING, NQ):
                    load(q)
                    maxima(q - 2)
                maxima(NQ - 2)
                maxima(NQ - 1)
                for t in range(TT):
                    sp.wait_ge(normed, TT * b + t + 1)
                    sp.dma_start(x_out[b, t * P:(t + 1) * P, :], y[:, t, :]).then_inc(x_stored, 16)
                    sp.wait_ge(tr_copied, TT * b + t + 1)
                    sp.dma_start(xt_out[b, :, :, t * P:(t + 1) * P],
                                 xtile[:, t % 2, :, :]).then_inc(xt_stored[t % 2], 16)

            with sp.Fori(0, B - 1) as b:
                body(b, True)
            body(B - 1, False)
            sp.wait_ge(x_stored, 16 * TT * B)
            sp.wait_ge(xt_stored[0], 8 * TT * B)
            sp.wait_ge(xt_stored[1], 8 * TT * B)

        @block.gpsimd
        def _(pool):
            pool.memset(vaug[:, :, :, D:D + 1], 1.0).then_inc(ones_set, 1)
            pool.wait_ge(ones_set, 1)
            pool.memset(ks[ROWS:P, :, :], 1.0).then_inc(ones_set, 1)
            pool.wait_ge(ones_set, 2)

            def body(b):
                for m in range(9):
                    if m < 8:
                        a = y[:, m % 2 * 2, :]
                        pool.wait_ge(rope_read, 24 * b + 3 * m + 3)
                        pool.tensor_tensor(a, a, y[:, m % 2 * 2 + 1, :], ALU.add).then_inc(rope_sum, 1)
                    if m >= 1:
                        a = y[:, (m - 1) % 2 * 2, :]
                        pool.wait_ge(plane_h, 8 * b + m)
                        pool.wait_ge(rope_sum, 8 * b + m)
                        pool.tensor_tensor(a, a, planes[:, (m - 1) % 2, 0, :], ALU.subtract).then_inc(rest_h, 1)
                for g in range(NQ // 2):
                    pool.wait_ge(at_hi_done, NQ // 2 * b + g + 1)
                    pool.tensor_tensor(at_lo[:, g, :], at[:, :], at_hi[:, g, :].bitcast(F32),
                                       ALU.subtract).then_inc(at_lo_done, 1)

            with pool.Fori(0, B) as b:
                body(b)

        @block.scalar
        def _(act):
            def body(b):
                for m in range(9):
                    if m < 8:
                        act.wait_ge(rope_sum, 8 * b + m + 1)
                        act.wait_ge(plane_out[m % 2], 64 * b + 16 * (m // 2))
                        act.activation(planes[:, m % 2, 0, :], y[:, m % 2 * 2, :], ACT.Copy).then_inc(plane_h, 1)
                    if m >= 1:
                        n = m - 1
                        act.wait_ge(rest_h, 8 * b + m)
                        act.activation(planes[:, n % 2, 1, :], y[:, n % 2 * 2, :], ACT.Copy).then_inc(plane_m, 1)
                        act.wait_ge(plane_m, 8 * b + m)
                        act.wait_ge(plane_l, 8 * b + m)
                        dst = (q_planes if n < 4 else k_planes)[b, n % 4]
                        act.dma_start(dst.rearrange("c p t -> p c t"), planes[:, n % 2, :, :]).then_inc(plane_out[n % 2], 16)
                act.wait_ge(ones_set, 2)
                act.wait_ge(pv_done, NQ * b)
                for t in range(TT):
                    act.wait_ge(proj_done, 12 * b + 8 + t + 1)
                    act.activation(vaug[:, t, :, 0:D], bank((8 + t) % 6).rearrange("p (h d) -> p h d", d=D),
                                   ACT.Copy).then_inc(v_copied, 1)

                def split_at(g):
                    act.wait_ge(at_ready, NQ // 2 * b + g + 1)
                    act.activation(at_hi[:, g, :], at[:, :], ACT.Copy).then_inc(at_hi_done, 1)

                for h in range(H):
                    act.wait_ge(st_done, H * b + h + 1)
                    if h >= PTR:
                        act.wait_ge(pv_done, NQ * b + (h - PTR) // QUAD + 1)
                    act.activation(pt[:, h % PTR, :], ps[1][:, 0:SC], ACT.Exp,
                                   scale=float(D) ** -0.5).then_inc(exp_done, 1)
                    if h % 8 == 3 and h > 8:
                        split_at(h // 8 - 1)
                split_at(NQ // 2 - 1)
                act.wait_ge(root_asked, b + 1)
                act.activation(small[:, 1, :], small[:, 0, :], ACT.Sqrt).then_inc(rooted, 1)
                for t in range(TT):
                    act.wait_ge(tr_done, TT * b + t + 1)
                    act.wait_ge(xt_stored[t % 2], 32 * b + 16 * (t // 2))
                    act.activation(xtile[:, t % 2, :, :], bank(4 + t % 2).rearrange("p (k t) -> p k t", k=KT),
                                   ACT.Copy).then_inc(tr_copied, 1)

            with act.Fori(0, B) as b:
                body(b)

        @block.vector
        def _(dve):
            dve.memset(pv[:, :], 0.0).then_inc(consts, 1)
            dve.wait_ge(const_in, 64)
            dve.tensor_copy(identb[:, :], ident[:, :]).then_inc(consts, 1)
            dve.tensor_copy(flat(masks), maskraw[:, :]).then_inc(consts, 1)
            for n in range(4):
                dve.wait_ge(w_loaded[n % 2], 16 * (n // 2 + 1))
                dve.tensor_copy(flat(w_hi[n]), wraw[:, n % 2, :]).then_inc(w_hi_done, 1)
                dve.wait_ge(w_hi_done, n + 1)
                dve.tensor_tensor(flat(w_lo[n]), wraw[:, n % 2, :], flat(w_hi[n]).bitcast(F32),
                                  ALU.subtract).then_inc(w_done, 1)

            def body(b):
                st = Steps(dve, dve_steps, b * DVE_PER, DVE_PER)
                dve.wait_ge(x_loaded, 16 * b + 16)
                dve.wait_ge(proj_done, 12 * b)
                dve.tensor_copy(flat(x_hi), flat(xraw)).then_inc(x_hi_done, 1)
                dve.wait_ge(x_hi_done, b + 1)
                dve.tensor_tensor(flat(x_lo), flat(xraw), flat(x_hi).bitcast(F32), ALU.subtract).then_inc(x_done, 1)
                dve.wait_ge(x_stored, 16 * TT * b)
                for m in range(9):
                    if m < 8:
                        a, c = y[:, m % 2 * 2, :], y[:, m % 2 * 2 + 1, :]
                        src = bank(m % 6)
                        dve.wait_ge(proj_done, 12 * b + m + 1)
                        dve.wait_ge(plane_l, 8 * b + max(m - 1, 0))
                        dve.tensor_tensor(a, src, cosr[:, :], ALU.mult).then_inc(rope_read, 1)
                        dve.tensor_tensor(c[0:64, :], src[64:P, :], sinr[0:64, :], ALU.mult).then_inc(rope_read, 1)
                        dve.tensor_tensor(c[64:P, :], src[0:64, :], sinr[64:P, :], ALU.mult).then_inc(rope_read, 1)
                    if m >= 1:
                        n = (m - 1) % 2
                        dve.wait_ge(plane_m, 8 * b + m)
                        dve.tensor_tensor(planes[:, n, 2, :], y[:, n * 2, :], planes[:, n, 1, :],
                                          ALU.subtract).then_inc(plane_l, 1)

                def norm_quad(q):
                    o = q % 2
                    dve.wait_ge(pv_done, NQ * b + q + 1)
                    dve.transpose(u[:, o, :, :].rearrange("p a b -> p (a b)"),
                                  pv[:, o * NB:(o + 1) * NB]).then_inc(pv_read, 1)
                    dve.wait_ge(pv_read, NQ * b + q + 1)
                    st.done(dve.reciprocal(rec[:, :], u[:, o, :, D]))
                    st.done(dve.tensor_tensor(un[:, :, o * D:(o + 1) * D], u[:, o, :, 0:D],
                                              rec[:, :].unsqueeze(2).to_broadcast([P, 16, D]), ALU.mult))
                    if o:
                        dve.wait_ge(at_lo_done, NQ // 2 * b + q // 2)
                        dve.transpose(at[:, :], flat(un)).then_inc(at_ready, 1)
                        dve.wait_ge(at_ready, NQ // 2 * b + q // 2 + 1)

                for h in range(H + LAG * QUAD + 2):
                    if h < H:
                        if h % QUAD == 0:
                            dve.wait_ge(qmax_done, NQ * b + h // QUAD)
                        dve.wait_ge(s_done, 2 * H * b + 2 * h + 1)
                        dve.tensor_reduce(bmax[:, h % QUAD, 8:10], ps[0][:, 2 * NB:SC].rearrange("p (a k) -> p a k", k=P),
                                          AX.X, ALU.max).then_inc(s_read, 1)
                        dve.wait_ge(s_done, 2 * H * b + 2 * h + 2)
                        dve.tensor_reduce(bmax[:, h % QUAD, 0:8], ps[0][:, 0:2 * NB].rearrange("p (a k) -> p a k", k=P),
                                          AX.X, ALU.max).then_inc(s_read, 1)
                    q = h // QUAD
                    if h % QUAD == QUAD - 1 and h < H:
                        dve.wait_ge(s_read, 2 * H * b + 2 * h + 2)
                        dve.wait_ge(maxt_done, NQ * b + q)
                        for i, (first, n) in enumerate(((7, 1), (8, 2), (4, 3), (0, 4))):
                            if i == 3:
                                st.wait()
                            ins = dve.tensor_reduce(qmax[:, :, i], bmax[:, :, first:first + n], AX.X, ALU.max)
                            if i == 3:
                                ins.then_inc(qmax_done, 1)
                            else:
                                st.inc(ins)
                    if h % QUAD == 0 and QUAD <= h <= H:
                        k = q - 1
                        dve.wait_ge(maxt_done, NQ * b + k + 1)
                        if k == 0:
                            dve.wait_ge(xt_stored[0], 8 * TT * b)
                        dve.tensor_scalar(mrest, maxt, -1.0, None, ALU.mult).then_inc(maxt_read, 1)
                        dve.wait_ge(maxt_read, NQ * b + k + 1)
                        if k >= 1:
                            dve.wait_ge(max_in[(k - 1) % 2], 48 * (NQ // 2 * b + (k - 1) // 2 + 1))
                        st.done(dve.tensor_copy(mplane[:, 0, :], mrest))
                        st.done(dve.tensor_tensor(mrest, mrest, mplane[:, 0, :], ALU.subtract))
                        st.done(dve.tensor_copy(mplane[:, 1, :], mrest))
                        dve.tensor_tensor(mplane[:, 2, :], mrest, mplane[:, 1, :],
                                          ALU.subtract).then_inc(max_split, 1)
                        dve.wait_ge(max_split, NQ * b + k + 1)
                    if h % QUAD == 1 and h >= QUAD * (LAG + 1) + 1:
                        norm_quad(h // QUAD - LAG - 1)
                dve.wait_ge(res_in, 16 * b + 16)
                for t in range(TT):
                    dve.wait_ge(o_done, TT * b + t + 1)
                    dve.tensor_tensor(y[:, t, :], bank(t), y[:, t, :], ALU.add).then_inc(o_read, 1)
                    dve.wait_ge(o_read, TT * b + t + 1)
                norm_rows(dve, st, y, stats, mv, small, root_asked, rooted, normed, b)
                st.end()

            with dve.Fori(0, B) as b:
                body(b)

        @block.tensor
        def _(pe):
            pe.wait_ge(consts, 3)

            def w(n, k, cols):
                return w_hi[n][:, k, cols], w_lo[n][:, k, cols]

            def x(k, cols):
                return x_hi[:, k, cols], x_lo[:, k, cols]

            def body(b):
                every = slice(0, T)
                pe.wait_ge(x_done, b + 1)
                pe.wait_ge(tr_copied, TT * b)
                for m in range(12):
                    if m >= 6:
                        pe.wait_ge(rope_read, 24 * b + 3 * (m - 5))
                    if m % 4 == 0:
                        pe.wait_ge(w_done, m // 4 + 1)
                    cols = slice(m % 4 * P, (m % 4 + 1) * P)
                    for k in range(KT):
                        if m < 8:
                            last = product3(pe, bank(m % 6), w(m // 4, k, cols), x(k, every), k == 0, k == KT - 1)
                        else:
                            last = product3(pe, bank(m % 6), x(k, cols), w(2, k, every), k == 0, k == KT - 1)
                    last.then_inc(proj_done, 1)

                def scores(h):
                    q, c0 = h // QUAD, h % QUAD * T
                    if h % QUAD == 0:
                        pe.wait_ge(stack_in[q % RING], 16 * LOADS * (NQ // RING * b + q // RING + 1))
                    def one(i, start):
                        return pe.matmul(ps[0][:, S_AT[i]:S_AT[i] + P * (i + 1)],
                                         qs[0:ROWS, q % RING, c0 + i * P:c0 + (i + 1) * P],
                                         ks[0:ROWS, q % RING, c0:c0 + P * (i + 1)],
                                         start=start, stop=False, skip_group_check=True)
                    def mask(a, n):
                        return pe.matmul(ps[0][:, a:a + n], identb[:, :], masks[:, 0, 0:n],
                                         start=False, stop=True, skip_group_check=True)
                    if h >= 1:
                        pe.wait_ge(s_read, 2 * H * b + 2 * h - 1)
                    if h % QUAD == 1 and h > 1:
                        pe.wait_ge(maxt_read, NQ * b + h // QUAD)
                    one(1, True)
                    mask(1152, P).then_inc(s_done, 1)
                    if h >= 1:
                        pe.wait_ge(s_read, 2 * H * b + 2 * h)
                    one(3, True)
                    mask(384, P)
                    one(2, True)
                    one(0, False)
                    mask(768, 2 * P).then_inc(s_done, 1)

                def scores_t(h):
                    q, c0 = h // QUAD, h % QUAD * T
                    if h % QUAD == 0:
                        pe.wait_ge(max_in[q % 2], 48 * (NQ // 2 * b + q // 2 + 1))
                    pe.wait_ge(exp_done, H * b + h)
                    rows = ROWS + 3
                    def one(j, start):
                        return pe.matmul(ps[1][:, ST_AT[j]:ST_AT[j] + T - P * j],
                                         ks[0:rows, q % RING, c0 + j * P:c0 + (j + 1) * P],
                                         qs[0:rows, q % RING, c0 + P * j:c0 + T],
                                         start=start, stop=False, skip_group_check=True)
                    def mask(a, n):
                        return pe.matmul(ps[1][:, a:a + n], identb[:, :], masks[:, 1, 0:n],
                                         start=False, stop=True, skip_group_check=True)
                    one(0, True)
                    mask(0, P)
                    one(3, True)
                    one(1, False)
                    mask(512, 2 * P)
                    one(2, True)
                    mask(1024, P).then_inc(st_done, 1)

                def values(q):
                    pe.wait_ge(exp_done, H * b + QUAD * (q + 1))
                    if q >= 2:
                        pe.wait_ge(pv_read, NQ * b + q - 1)
                    c = q % 2 * NB
                    for j in range(TT):
                        for g in range(QUAD):
                            h = QUAD * q + g
                            last = pe.matmul(pv[32 * g:32 * g + D + 1, c + j * P:c + T], vaug[:, j, h, :],
                                             pt[:, h % PTR, ST_AT[j]:ST_AT[j] + T - P * j],
                                             start=j == 0, stop=j == TT - 1)
                    last.then_inc(pv_done, 1)

                pe.wait_ge(rope_read, 24 * b + 24)
                pe.wait_ge(v_copied, TT * b + TT)
                for h in range(H + LAG * QUAD + 1):
                    if h < H:
                        scores(h)
                    if h % QUAD == 0 and QUAD <= h <= H:
                        pe.wait_ge(qmax_done, NQ * b + h // QUAD)
                        pe.wait_ge(s_read, 2 * H * b + 2 * min(h + 1, H) - 1)
                        pe.transpose(maxt, qmax[:, :, :].rearrange("p h i -> p (h i)"), ident[:, :]).then_inc(maxt_done, 1)
                    if h >= LAG * QUAD:
                        n = h - LAG * QUAD
                        if n < H:
                            scores_t(n)
                        if n % QUAD == 0 and n >= QUAD:
                            values(n // QUAD - 1)
                pe.wait_ge(w_done, 4)
                pe.wait_ge(s_read, 2 * H * (b + 1))
                pe.wait_ge(maxt_read, NQ * (b + 1))
                pe.wait_ge(exp_done, H * (b + 1))
                for g in range(NQ // 2):
                    pe.wait_ge(at_lo_done, NQ // 2 * b + g + 1)
                    for t in range(TT):
                        cols = slice(t * P, (t + 1) * P)
                        last = product3(pe, bank(t), (at_hi[:, g, cols], at_lo[:, g, cols]), w(3, g, every),
                                        g == 0, g == NQ // 2 - 1)
                        if g == NQ // 2 - 1:
                            last.then_inc(o_done, 1)
                for t in range(TT):
                    pe.wait_ge(normed, TT * b + t + 1)
                    if t >= 2:
                        pe.wait_ge(tr_copied, TT * b + t - 1)
                    for k in range(KT):
                        last = pe.transpose(bank(4 + t % 2)[:, k * P:(k + 1) * P], y[:, t, k * P:(k + 1) * P], ident[:, :])
                    last.then_inc(tr_done, 1)

            with pe.Fori(0, B) as b:
                body(b)


CH = 896
CHUNKS = KT * F // CH


def gated_ffn_phase(nc, tag, x_in, xt_in, pairs, ident_in, x_out, xt_out):
    with ExitStack() as ctx:
        def sb(name, shape, dt=F32, at=ctx):
            return at.enter_context(nc.sbuf_tensor(f"{tag}_{name}", shape, dt))

        def sem(name):
            return ctx.enter_context(nc.semaphore(f"{tag}_{name}"))

        w_hi = [sb(f"w{n}_hi", s, F32R) for n, s in enumerate(([P, KT, F], [P, KT, F], [P, FT, C]))]
        w_lo = [sb(f"w{n}_lo", s, F32R) for n, s in enumerate(([P, KT, F], [P, KT, F], [P, FT, C]))]
        with ExitStack() as early:
            raw = sb("raw", [P, 2, 2, CH], at=early)
            made = sb("made", [P, 2, CH], at=early)
            sums = sb("sums", [P, 3, CHUNKS], at=early)
            total = sb("total", [P, 3], at=early)
            ones = sb("ones", [P, P], at=early)
        y = sb("y", [P, TT, T])
        x_hi = sb("x_hi", [P, KT, T], F32R)
        x_lo = sb("x_lo", [P, KT, T], F32R)
        gate = sb("gate", [P, 2, T])
        h = sb("h", [P, T])
        h_hi = sb("h_hi", [P, 2, T], F32R)
        h_lo = sb("h_lo", [P, 2, T], F32R)
        coeff = sb("coeff", [P, 3])
        ident = sb("ident", [P, P])
        stats = sb("stats", [P, TT, 6])
        mv = sb("mv", [P, TT, 2])
        small = sb("small", [P, 4, TT])
        ps = ctx.enter_context(nc.psum_tensor(f"{tag}_ps", [P, 8, NB], F32))

        raw_in, raw_read, diff_done = [sem("raw_in0"), sem("raw_in1")], sem("raw_read"), sem("diff_done")
        abs_done, sum_done, total_done, coeff_done = sem("abs_done"), sem("sum_done"), sem("total_done"), sem("coeff_done")
        sign_done, w_made, w_hi_done, w_done = sem("sign_done"), sem("w_made"), sem("w_hi_done"), sem("w_done")
        ones_set, ident_set = sem("ones_set"), sem("ident_set")
        x_loaded, x_hi_done, x_done, x_read = sem("x_loaded"), sem("x_hi_done"), sem("x_done"), sem("x_read")
        up_done, silu_done, h_done, h_hi_done, h_lo_done, down_done = (
            sem("up_done"), sem("silu_done"), sem("h_done"), sem("h_hi_done"), sem("h_lo_done"), sem("down_done"))
        res_in, o_read = sem("res_in"), sem("o_read")
        root_asked, rooted, normed = sem("root_asked"), sem("rooted"), sem("normed")
        tr_done, tr_copied, x_stored = sem("tr_done"), sem("tr_copied"), sem("x_stored")
        xt_stored = [sem("xt_stored0"), sem("xt_stored1")]
        dve_steps = sem("dve_steps")
        block = ctx.enter_context(nc.Block())
        N = 3 * CHUNKS

        def part(ap, c):
            return ap.rearrange("p k n -> p (k n)")[:, c * CH:(c + 1) * CH]

        @block.sync
        def _(sp):
            for i in range(2 * N):
                n, c = i % N // CHUNKS, i % CHUNKS
                if i >= 2:
                    sp.wait_ge(raw_read, i - 1)
                for s in range(2):
                    sp.dma_start(raw[:, i % 2, s, :], part(pairs[n][s], c)).then_inc(raw_in[i % 2], 16)
            sp.wait_ge(w_done, N)
            sp.dma_start(ident[:, :], ident_in).then_inc(ident_set, 16)

            def body(b):
                sp.wait_ge(x_stored, 16 * TT * b)
                sp.dma_start(y[:, :, :], xt_in[b]).then_inc(x_loaded, 16)
                sp.wait_ge(x_done, b + 1)
                sp.dma_start(y[:, :, :], x_in[b].rearrange("(t p) c -> p t c", p=P)).then_inc(res_in, 16)
                for t in range(TT):
                    sp.wait_ge(normed, TT * b + t + 1)
                    sp.dma_start(x_out[b, t * P:(t + 1) * P, :], y[:, t, :]).then_inc(x_stored, 16)
                    sp.wait_ge(tr_copied, TT * b + t + 1)
                    sp.dma_start(xt_out[b, :, :, t * P:(t + 1) * P],
                                 gate[:, t % 2, :].rearrange("p (k t) -> p k t", k=KT)).then_inc(xt_stored[t % 2], 16)

            with sp.Fori(0, B) as b:
                body(b)
            sp.wait_ge(x_stored, 16 * TT * B)
            sp.wait_ge(xt_stored[0], 8 * TT * B)
            sp.wait_ge(xt_stored[1], 8 * TT * B)

        @block.scalar
        def _(act):
            for i in range(N):
                act.wait_ge(diff_done, i + 1)
                act.activation(made[:, i % 2, :], made[:, i % 2, :], ACT.Abs,
                               accum_out=sums[:, i // CHUNKS, i % CHUNKS:i % CHUNKS + 1]).then_inc(abs_done, 1)
            for i in range(N):
                act.wait_ge(diff_done, N + i + 1)
                act.activation(made[:, i % 2, :], made[:, i % 2, :], ACT.Sign).then_inc(sign_done, 1)
                act.wait_ge(w_made, i + 1)
                act.activation(part(w_hi[i // CHUNKS][:, :, :], i % CHUNKS), made[:, i % 2, :], ACT.Copy).then_inc(w_hi_done, 1)

            def body(b):
                for f in range(FT):
                    n = FT * b + f
                    act.wait_ge(up_done, 2 * n + 1)
                    act.wait_ge(h_done, max(f - 1, 0) + FT * b)
                    if f == 0:
                        act.wait_ge(xt_stored[0], 32 * b)
                        act.wait_ge(xt_stored[1], 32 * b)
                    act.activation(gate[:, f % 2, :], ps[:, 4 + f % 2 * 2, :], ACT.Silu).then_inc(silu_done, 1)
                    act.wait_ge(h_done, n + 1)
                    act.wait_ge(down_done, FT * b + max(f - 1, 0))
                    act.activation(h_hi[:, f % 2, :], h[:, :], ACT.Copy).then_inc(h_hi_done, 1)
                act.wait_ge(root_asked, b + 1)
                act.activation(small[:, 1, :], small[:, 0, :], ACT.Sqrt).then_inc(rooted, 1)
                for t in range(TT):
                    act.wait_ge(tr_done, TT * b + t + 1)
                    act.wait_ge(xt_stored[t % 2], 32 * b + 16 * (t // 2))
                    act.activation(gate[:, t % 2, :], ps[:, 4 + t % 2, :], ACT.Copy).then_inc(tr_copied, 1)

            with act.Fori(0, B) as b:
                body(b)

        DVE_PER = NORM_STEPS

        @block.vector
        def _(dve):
            dve.memset(ones[:, :], 1.0).then_inc(ones_set, 1)
            for i in range(2 * N):
                dve.wait_ge(raw_in[i % 2], 32 * (i // 2 + 1))
                j = i - N
                if i < N and i >= 2:
                    dve.wait_ge(abs_done, i - 1)
                if j in (0, 1):
                    dve.wait_ge(abs_done, N)
                if j >= 2:
                    dve.wait_ge(w_done, j - 1)
                dve.tensor_tensor(made[:, i % 2, :], raw[:, i % 2, 0, :], raw[:, i % 2, 1, :], ALU.subtract).then_inc(diff_done, 1)
                if i < N:
                    dve.wait_ge(diff_done, i + 1)
                    dve.sem_inc(raw_read, 1)
                if i == N - 1:
                    dve.wait_ge(abs_done, N)
                    dve.tensor_reduce(total[:, :], sums[:, :, :], AX.X, ALU.add).then_inc(sum_done, 1)
                    dve.wait_ge(total_done, 1)
                    dve.tensor_scalar(coeff[:, :], ps[:, 0, 0:3], 1.0 / (C * F), None, ALU.mult).then_inc(coeff_done, 1)
                    dve.wait_ge(coeff_done, 1)
                if j >= 0:
                    n = j // CHUNKS
                    dve.wait_ge(sign_done, j + 1)
                    dve.scalar_tensor_tensor(out=made[:, i % 2, :], in0=made[:, i % 2, :], scalar=coeff[:, n:n + 1],
                                             in1=raw[:, i % 2, 1, :], op0=ALU.mult, op1=ALU.add).then_inc(w_made, 1)
                    dve.wait_ge(w_made, j + 1)
                    dve.sem_inc(raw_read, 1)
                    dve.wait_ge(w_hi_done, j + 1)
                    dve.tensor_tensor(part(w_lo[n][:, :, :], j % CHUNKS), made[:, i % 2, :],
                                      part(w_hi[n][:, :, :], j % CHUNKS).bitcast(F32), ALU.subtract).then_inc(w_done, 1)

            def body(b):
                st = Steps(dve, dve_steps, b * DVE_PER, DVE_PER)
                dve.wait_ge(x_loaded, 16 * b + 16)
                dve.wait_ge(up_done, 2 * FT * b)
                dve.tensor_copy(flat(x_hi), flat(y)).then_inc(x_hi_done, 1)
                dve.wait_ge(x_hi_done, b + 1)
                dve.tensor_tensor(flat(x_lo), flat(y), flat(x_hi).bitcast(F32), ALU.subtract).then_inc(x_done, 1)
                for f in range(FT):
                    n = FT * b + f
                    dve.wait_ge(silu_done, n + 1)
                    dve.wait_ge(up_done, 2 * n + 2)
                    dve.wait_ge(h_lo_done, n)
                    dve.tensor_tensor(h[:, :], ps[:, 5 + f % 2 * 2, :], gate[:, f % 2, :], ALU.mult).then_inc(h_done, 1)
                    dve.wait_ge(h_hi_done, n + 1)
                    dve.tensor_tensor(h_lo[:, f % 2, :], h[:, :], h_hi[:, f % 2, :].bitcast(F32), ALU.subtract).then_inc(h_lo_done, 1)
                dve.wait_ge(down_done, FT * (b + 1))
                dve.wait_ge(res_in, 16 * b + 16)
                for t in range(TT):
                    dve.tensor_tensor(y[:, t, :], ps[:, t, :], y[:, t, :], ALU.add).then_inc(o_read, 1)
                    dve.wait_ge(o_read, TT * b + t + 1)
                norm_rows(dve, st, y, stats, mv, small, root_asked, rooted, normed, b)
                st.end()

            with dve.Fori(0, B) as b:
                body(b)

        @block.tensor
        def _(pe):
            pe.wait_ge(ones_set, 1)
            pe.wait_ge(sum_done, 1)
            pe.matmul(ps[:, 0, 0:3], ones[:, :], total[:, :], start=True, stop=True).then_inc(total_done, 1)
            pe.wait_ge(coeff_done, 1)
            pe.wait_ge(w_done, N)
            pe.wait_ge(ident_set, 16)

            def body(b):
                def up(f):
                    if f >= 2:
                        pe.wait_ge(h_done, FT * b + f - 1)
                    cols = slice(f * P, (f + 1) * P)
                    for m in range(2):
                        for k in range(KT):
                            last = product3(pe, ps[:, 4 + f % 2 * 2 + m, :], (w_hi[m][:, k, cols], w_lo[m][:, k, cols]),
                                            (x_hi[:, k, :], x_lo[:, k, :]), k == 0, k == KT - 1)
                        last.then_inc(up_done, 1)

                def down(f):
                    pe.wait_ge(h_lo_done, FT * b + f + 1)
                    if f == 0:
                        pe.wait_ge(o_read, TT * b)
                    for t in range(TT):
                        cols = slice(t * P, (t + 1) * P)
                        last = product3(pe, ps[:, t, :], (h_hi[:, f % 2, cols], h_lo[:, f % 2, cols]),
                                        (w_hi[2][:, f, :], w_lo[2][:, f, :]), f == 0, f == FT - 1)
                    last.then_inc(down_done, 1)

                pe.wait_ge(x_done, b + 1)
                pe.wait_ge(tr_copied, TT * b)
                for f in range(FT):
                    up(f)
                    if f:
                        down(f - 1)
                down(FT - 1)
                for t in range(TT):
                    pe.wait_ge(normed, TT * b + t + 1)
                    if t >= 2:
                        pe.wait_ge(tr_copied, TT * b + t - 1)
                    for k in range(KT):
                        last = pe.transpose(ps[:, 4 + t % 2, k * P:(k + 1) * P], y[:, t, k * P:(k + 1) * P], ident[:, :])
                    last.then_inc(tr_done, 1)

            with pe.Fori(0, B) as b:
                body(b)


def quantised_ffn_phase(nc, tag, x_in, xt_in, w_idx, absmax, bias, out):
    HALF = P // 2
    with ExitStack() as ctx:
        def sb(name, shape, dt=F32):
            return ctx.enter_context(nc.sbuf_tensor(f"{tag}_{name}", shape, dt))

        def sem(name):
            return ctx.enter_context(nc.semaphore(f"{tag}_{name}"))

        idx = sb("idx", [P, KT, C], I32)
        code = sb("code", [P, 2, KT * C])
        w = sb("w", [P, KT, C])
        scale = sb("scale", [P, KT, C])
        w_hi = sb("w_hi", [P, KT, C], F32R)
        w_lo = sb("w_lo", [P, KT, C], F32R)
        biasr = sb("biasr", [P, C])
        xraw = sb("xraw", [P, 2, KT * T])
        x_hi = sb("x_hi", [P, 2, KT, T], F32R)
        x_lo = sb("x_lo", [P, 2, KT, T], F32R)
        y = sb("y", [P, 2, TT, T])
        stats = sb("stats", [P, TT, 6])
        mv = sb("mv", [P, TT, 2])
        small = sb("small", [P, 4, TT])
        ps = ctx.enter_context(nc.psum_tensor(f"{tag}_ps", [P, 8, NB], F32))

        w_in, code_done, w_step, w_hi_done, w_done = sem("w_in"), sem("code_done"), sem("w_step"), sem("w_hi_done"), sem("w_done")
        x_loaded, x_hi_done, x_done = [sem("x_loaded0"), sem("x_loaded1")], sem("x_hi_done"), sem("x_done")
        res_in, biased, o_done, o_read = [sem("res_in0"), sem("res_in1")], sem("biased"), sem("o_done"), sem("o_read")
        root_asked, rooted, normed = sem("root_asked"), sem("rooted"), sem("normed")
        stored, dve_steps = [sem("stored0"), sem("stored1")], sem("dve_steps")
        block = ctx.enter_context(nc.Block())

        @block.sync
        def _(sp):
            sp.dma_start(idx[:, :, :], w_idx).then_inc(w_in, 16)
            for half in range(2):
                sp.dma_start(scale[half * HALF:(half + 1) * HALF, :, :],
                             absmax[half:half + 1].to_broadcast([HALF, KT, C])).then_inc(w_in, 16)
            sp.dma_start(biasr[:, :], bias.to_broadcast([P, C])).then_inc(w_in, 16)
            for b in range(B):
                i = b % 2
                if b >= 2:
                    sp.wait_ge(x_done, b - 1)
                    sp.wait_ge(stored[i], 16 * TT * (b // 2))
                sp.dma_start(xraw[:, i, :], xt_in[b].rearrange("p k t -> p (k t)")).then_inc(x_loaded[i], 16)
                sp.dma_start(y[:, i, :, :], x_in[b].rearrange("(t p) c -> p t c", p=P)).then_inc(res_in[i], 16)

        @block.gpsimd
        def _(pool):
            for b in range(B):
                pool.wait_ge(w_in, 64)
                pool.wait_ge(res_in[b % 2], 16 * (b // 2 + 1))
                for t in range(TT):
                    pool.tensor_tensor(y[:, b % 2, t, :], y[:, b % 2, t, :], biasr[:, :], ALU.add).then_inc(biased, 1)

        @block.scalar
        def _(act):
            for b in range(B):
                act.wait_ge(root_asked, b + 1)
                act.activation(small[:, 1, :], small[:, 0, :], ACT.Sqrt).then_inc(rooted, 1)
                for t in range(TT):
                    act.wait_ge(normed, TT * b + t + 1)
                    act.dma_start(out[b, t * P:(t + 1) * P, :], y[:, b % 2, t, :]).then_inc(stored[b % 2], 16)
            act.wait_ge(stored[0], 16 * TT * B // 2)
            act.wait_ge(stored[1], 16 * TT * B // 2)

        @block.vector
        def _(dve):
            dve.wait_ge(w_in, 64)
            i_flat, w_flat = flat(idx), flat(w)
            for c, value in enumerate(NF4):
                if c == 0:
                    dve.tensor_scalar(w_flat, i_flat, 0.0, NF4[0], ALU.is_equal, ALU.mult).then_inc(w_step, 1)
                    continue
                dve.wait_ge(w_step, max(c - 1, 1))
                dve.tensor_scalar(code[:, c % 2, :], i_flat, float(c), value, ALU.is_equal, ALU.mult).then_inc(code_done, 1)
                dve.wait_ge(code_done, c)
                dve.wait_ge(w_step, c)
                dve.tensor_tensor(w_flat, w_flat, code[:, c % 2, :], ALU.add).then_inc(w_step, 1)
            n = len(NF4)
            dve.wait_ge(w_step, n)
            dve.tensor_tensor(w_flat, w_flat, flat(scale), ALU.mult).then_inc(w_step, 1)
            dve.wait_ge(w_step, n + 1)
            dve.tensor_copy(flat(w_hi), w_flat).then_inc(w_hi_done, 1)
            dve.wait_ge(w_hi_done, 1)
            dve.tensor_tensor(flat(w_lo), w_flat, flat(w_hi).bitcast(F32), ALU.subtract).then_inc(w_done, 1)

            def split(b):
                i = b % 2
                dve.wait_ge(x_loaded[i], 16 * (b // 2 + 1))
                if b >= 2:
                    dve.wait_ge(o_done, TT * (b - 1))
                hi, lo = x_hi[:, i, :, :].rearrange("p k t -> p (k t)"), x_lo[:, i, :, :].rearrange("p k t -> p (k t)")
                dve.tensor_copy(hi, xraw[:, i, :]).then_inc(x_hi_done, 1)
                dve.wait_ge(x_hi_done, b + 1)
                dve.tensor_tensor(lo, xraw[:, i, :], hi.bitcast(F32), ALU.subtract).then_inc(x_done, 1)

            split(0)
            for b in range(B):
                if b + 1 < B:
                    split(b + 1)
                st = Steps(dve, dve_steps, b * NORM_STEPS, NORM_STEPS)
                dve.wait_ge(biased, TT * (b + 1))
                for t in range(TT):
                    dve.wait_ge(o_done, TT * b + t + 1)
                    dve.tensor_tensor(y[:, b % 2, t, :], ps[:, b % 2 * TT + t, :], y[:, b % 2, t, :], ALU.add).then_inc(o_read, 1)
                    dve.wait_ge(o_read, TT * b + t + 1)
                norm_rows(dve, st, y[:, b % 2, :, :], stats, mv, small, root_asked, rooted, normed, b)
                st.end()

        @block.tensor
        def _(pe):
            pe.wait_ge(w_done, 1)
            for b in range(B):
                pe.wait_ge(x_done, b + 1)
                if b >= 2:
                    pe.wait_ge(o_read, TT * (b - 1))
                for t in range(TT):
                    cols = slice(t * P, (t + 1) * P)
                    for k in range(KT):
                        last = product3(pe, ps[:, b % 2 * TT + t, :], (x_hi[:, b % 2, k, cols], x_lo[:, b % 2, k, cols]),
                                        (w_hi[:, k, :], w_lo[:, k, :]), k == 0, k == KT - 1)
                    last.then_inc(o_done, 1)


def head_channels(order):
    rows = []
    for tile in range(C // P):
        for d in range(D):
            half, i = d // (D // 2), d % (D // 2)
            within = 2 * i + half if order == "pairs" else half * (D // 2) + i
            rows += [(tile * 2 * QUAD + h) * D + within for h in range(2 * QUAD)]
    return np.array(rows)


def output_channels():
    return np.array([((2 * g + o) * QUAD + h) * D + d
                     for g in range(NQ // 2) for h in range(QUAD) for o in range(2) for d in range(D)])


def rotary(order):
    f = np.float32
    t = np.arange(T, dtype=f)
    if order == "pairs":
        freqs = np.ones(D // 2, f)
    else:
        freqs = (f(1.0) / np.power(f(10000.0), np.arange(0, D, 2, dtype=f) / f(D))).astype(f)
    theta = (t[None, :] * freqs[:, None]).astype(f).astype(np.float64)
    cos = np.repeat(np.concatenate([np.cos(theta)] * 2), 2 * QUAD, axis=0).astype(f)
    sin = np.repeat(np.concatenate([-np.sin(theta), np.sin(theta)]), 2 * QUAD, axis=0).astype(f)
    return cos, sin


def by_partition(w):
    k, n = w.shape
    return np.ascontiguousarray(w.reshape(k // P, P, n).transpose(1, 0, 2))


def causal_masks():
    later = np.triu(np.ones((P, P)), 1) * -1e30
    return np.concatenate([later, later, later.T, later.T], axis=1).astype(np.float32)


def two_layers(nc, x, xt, l0, ffn, l1, rope0, rope1, ident, masks, w_idx, absmax, bias, out):
    def rows(name):
        return nc.dram_tensor(name, [B, T, C], F32).ap()

    def channels(name):
        return nc.dram_tensor(name, [B, P, KT, T], F32).ap()

    q_planes = nc.dram_tensor("q_planes", [B, C // P, 3, P, T], BF16).ap()
    k_planes = nc.dram_tensor("k_planes", [B, C // P, 3, P, T], BF16).ap()
    x1, x1t, x2, x2t, x3, x3t = rows("x1"), channels("x1t"), rows("x2"), channels("x2t"), rows("x3"), channels("x3t")
    attention_phase(nc, "a0", x, xt, l0, *rope0, ident, masks, x1, x1t, q_planes, k_planes)
    gated_ffn_phase(nc, "f0", x1, x1t, ffn, ident, x2, x2t)
    attention_phase(nc, "a1", x2, x2t, l1, *rope1, ident, masks, x3, x3t, q_planes, k_planes)
    quantised_ffn_phase(nc, "f1", x3, x3t, w_idx, absmax, bias, out)


def kernel(**inputs):
    import concourse.bacc as bacc
    from concourse.bass_utils import run_bass_kernel_spmd

    g = {n: np.asarray(a) for n, a in inputs.items()}
    x = g["L0_attn_x"]
    arrays = {
        "x": x,
        "xt": np.ascontiguousarray(x.transpose(0, 2, 1).reshape(B, KT, P, T).transpose(0, 2, 1, 3)),
    }
    for layer, order in ((0, "pairs"), (1, "halves")):
        ch = head_channels(order)
        for n in "qk":
            arrays[f"w{n}{layer}"] = by_partition(g[f"L{layer}_attn_w{n}"][ch].T)
        arrays[f"wv{layer}"] = by_partition(g[f"L{layer}_attn_wv"].T)
        arrays[f"wo{layer}"] = by_partition(g[f"L{layer}_attn_wo"].T[output_channels()])
        arrays[f"cos{layer}"], arrays[f"sin{layer}"] = rotary(order)
    for n in (1, 3, 2):
        arrays[f"w{n}"] = by_partition(g[f"L0_ffn_w{n}"].T)
        arrays[f"mean_w{n}"] = by_partition(g[f"L0_ffn_mean_w{n}"].T)
    arrays["ident"] = np.eye(P, dtype=np.float32)
    arrays["masks"] = causal_masks()
    arrays["w_idx"] = by_partition(g["L1_ffn_w_idx"].T)
    arrays["absmax"] = np.ascontiguousarray(g["L1_ffn_absmax"].reshape(C, KT, 2).transpose(2, 1, 0))
    arrays["bias"] = g["L1_ffn_bias"].reshape(1, C)

    nc = bacc.Bacc("TRN2", target_bir_lowering=False, num_devices=1)
    arrays = {f"in_{n}": np.ascontiguousarray(a) for n, a in arrays.items()}
    t = {n[3:]: nc.dram_tensor(n, a.shape, mybir.dt.from_np(a.dtype), kind="ExternalInput").ap()
         for n, a in arrays.items()}
    out = nc.dram_tensor("out", (B, T, C), F32, kind="ExternalOutput").ap()
    two_layers(nc, t["x"], t["xt"], [t[f"w{n}0"] for n in "qkvo"],
               [(t[f"w{n}"], t[f"mean_w{n}"]) for n in (1, 3, 2)], [t[f"w{n}1"] for n in "qkvo"],
               (t["cos0"], t["sin0"]), (t["cos1"], t["sin1"]), t["ident"], t["masks"],
               t["w_idx"], t["absmax"], t["bias"], out)
    r = run_bass_kernel_spmd(nc, [arrays], core_ids=[0])
    return r.results[0]["out"]
```

```python
from contextlib import ExitStack

import numpy as np

import concourse.bass as bass
from concourse import mybir

ALU = mybir.AluOpType
ACT = mybir.ActivationFunctionType
AX = mybir.AxisListType
F32 = mybir.dt.float32
F32R = mybir.dt.float32r
BF16 = mybir.dt.bfloat16
I32 = mybir.dt.int32

P = 128
B, T, C = 4, 512, 512
H = 32
D = C // H
KT = C // P
TT = T // P
F = 1792
FT = F // P
NB = 512
QUAD = 4
NQ = H // QUAD
RING = 4
PTR = 7
LAG = 7
LAST = H + LAG + QUAD + 3
TR_AT = (0, 1, 4, 5)
NSLOT = 6
ROWS = NSLOT * D
SC = T + 384 + 256 + 128
S_AT = {3: 0, 2: 512, 0: 896, 1: 1024}
ST_AT = {0: 0, 3: 512, 1: 640, 2: 1024}
EPS = 1e-5
NF4 = [-1.0, -0.6961928009986877, -0.5250730514526367, -0.39491748809814453, -0.28444138169288635,
       -0.18477343022823334, -0.09105003625154495, 0.0, 0.07958029955625534, 0.16093020141124725,
       0.24611230194568634, 0.33791524171829224, 0.44070982933044434, 0.5626170039176941,
       0.7229568362236023, 1.0]



class Steps:

    def __init__(self, eng, sem, base, per):
        self.eng, self.sem, self.base, self.per, self.n = eng, sem, base, per, 0

    def inc(self, ins):
        ins.then_inc(self.sem, 1)
        self.n += 1

    def wait(self):
        self.eng.wait_ge(self.sem, self.base + self.n)

    def done(self, ins):
        self.inc(ins)
        self.wait()

    def end(self):
        assert self.n == self.per, (self.n, self.per)


def product3(eng, out, lhs, rhs, start=True, stop=True):
    (lh, ll), (rh, rl) = lhs, rhs
    eng.matmul(out, lh, rh, start=start, stop=False)
    eng.matmul(out, lh, rl, start=False, stop=False)
    return eng.matmul(out, ll, rh, start=False, stop=stop)


def at_least(eng, sem, value):
    if not (isinstance(value, int) and value == 0):
        eng.wait_ge(sem, value)


def hold(eng, sem):
    eng.sem_inc(sem, 1)


NORM_STEPS = 2 * TT + 5


def norm_rows(dve, st, y, stats, mv, small, root_asked, rooted, normed, b):
    for t in range(TT):
        st.inc(dve.bn_stats(stats[:, t, :], y[:, t, :]))
    st.wait()
    dve.memset(small[:, 2, :], 0.0)
    for t in range(TT):
        st.inc(dve.bn_aggr(mv[:, t, :], stats[:, t, :]))
    st.wait()
    dve.tensor_scalar(small[:, 0, :], mv[:, :, 1], EPS, None, ALU.add).then_inc(root_asked, 1)
    dve.wait_ge(rooted, b + 1)
    dve.wait_ge(root_asked, b + 1)
    v, s, r = small[:, 0, :], small[:, 1, :], small[:, 2, :]
    st.done(dve.reciprocal(r, s))
    st.done(dve.tensor_tensor(r, r, v, ALU.mult))
    st.done(dve.tensor_tensor(r, r, s, ALU.add))
    st.done(dve.tensor_scalar(r, r, 0.5, None, ALU.mult))
    st.done(dve.reciprocal(small[:, 3, :], r))
    for t in range(TT):
        dve.tensor_scalar(y[:, t, :], y[:, t, :], mv[:, t, 0:1], small[:, 3, t:t + 1],
                          ALU.subtract, ALU.mult).then_inc(normed, 1)


def flat(ap):
    return ap[:, :, :].rearrange("p a b -> p (a b)")


def attention_phase(nc, tag, x_in, xt_in, wts, cos_in, sin_in, ident_in, mask_in, x_out, xt_out,
                    q_planes, k_planes):
    split_x = len(xt_in) == 1
    with ExitStack() as ctx:
        def sb(name, shape, dt=F32, at=ctx):
            return at.enter_context(nc.sbuf_tensor(f"{tag}_{name}", shape, dt))

        def sem(name):
            return nc.alloc_semaphore(f"{tag}_{name}")

        w_hi = [sb(f"w{n}_hi", [P, KT, C], F32R) for n in "qkvo"]
        w_lo = [sb(f"w{n}_lo", [P, KT, C], F32R) for n in "qkvo"]
        x_hi = sb("x_hi", [P, KT, T], F32R)
        x_lo = sb("x_lo", [P, KT, T], F32R)
        vaug = sb("vaug", [P, TT, H, D + 1])
        cosr = sb("cosr", [P, T])
        sinr = sb("sinr", [P, T])
        qs = sb("qs", [P, RING, QUAD * T], BF16)
        ks = sb("ks", [P, RING, QUAD * T], BF16)
        u = sb("u", [P, 2, T])
        un = sb("un", [P, 16, 32])
        at = sb("at", [P, T])
        rec = sb("rec", [P, 2, 16])
        tile_hi = sb("tile_hi", [P, 2, KT, P], F32R)
        tile_lo = sb("tile_lo", [P, 2, KT, P], F32R)
        ident = sb("ident", [P, P])
        identb = sb("identb", [P, P], BF16)
        masks = sb("masks", [P, 2, 2 * P], BF16)
        bmax = sb("bmax", [P, QUAD, 10])
        qmax = sb("qmax", [P, QUAD, TT])
        mplane = sb("mplane", [QUAD * TT, 3, P], BF16)
        mrest = sb("mrest", [QUAD * TT, P])
        stats = sb("stats", [P, TT, 6])
        mv = sb("mv", [P, TT, 2])
        small = sb("small", [P, 4, TT])
        with ExitStack() as early:
            xraw = sb("xraw", [P, KT * T], at=early)
            wraw = sb("wraw", [P, 2, KT * C], at=early)
            maskraw = sb("maskraw", [P, 4 * P], at=early)
        at_hi = sb("at_hi", [P, NQ // 2, T], F32R)
        at_lo = sb("at_lo", [P, NQ // 2, T], F32R)
        y = sb("y", [P, TT, T])
        pt = sb("pt", [P, PTR, SC])
        RR = 4

        def planes(m, i=None):
            v = pt[:, m % RR, 0:3 * T // 2].bitcast(BF16).rearrange("p (c t) -> p c t", c=3)
            return v if i is None else v[:, i, :]

        def rope_a(m):
            return pt[:, m % RR, 3 * T // 2:3 * T // 2 + T]

        def rope_b(m):
            return u[:, m % 2, :]

        ps = [ctx.enter_context(nc.psum_tensor(f"{tag}_ps{i}", [P, 3 * NB], F32)) for i in range(2)]
        pv = ctx.enter_context(nc.psum_tensor(f"{tag}_pv", [P, 2 * NB], F32))

        def bank(n):
            return ps[n // 3][:, (n % 3) * NB:(n % 3 + 1) * NB]

        def v_bank(t):
            return bank((3, 4, 5, 2)[t])

        maxt = ps[0][0:QUAD * TT, SC:SC + P]

        w_loaded = [sem("w_loaded0"), sem("w_loaded1")]
        w_hi_done, w_done = sem("w_hi_done"), sem("w_done")
        const_in, consts, ones_set = sem("const_in"), sem("consts"), sem("ones_set")
        xraw_in, x_hi_done, x_split = sem("xraw_in"), sem("x_hi_done"), sem("x_split")
        x_loaded, proj_done, rope_read, v_copied = sem("x_loaded"), sem("proj_done"), sem("rope_read"), sem("v_copied")
        rope_sum, plane_h, rest_h, plane_m, plane_l = (
            sem("rope_sum"), sem("plane_h"), sem("rest_h"), sem("plane_m"), sem("plane_l"))
        plane_out = [sem(f"plane_out{i}") for i in range(RR)]
        stack_in = [sem(f"stack_in{r}") for r in range(RING)]
        s_done, s_read, qmax_done, maxt_done = sem("s_done"), sem("s_read"), sem("qmax_done"), sem("maxt_done")
        maxt_read, max_split, max_step = sem("maxt_read"), sem("max_split"), sem("max_step")
        max_in = [sem("max_in0"), sem("max_in1")]
        st_done, exp_done, pv_done, pv_read = sem("st_done"), sem("exp_done"), sem("pv_done"), sem("pv_read")
        rec_done, un_done = sem("rec_done"), sem("un_done")
        at_ready, at_hi_done, at_lo_done = sem("at_ready"), sem("at_hi_done"), sem("at_lo_done")
        res_in, o_done, o_read = sem("res_in"), sem("o_done"), sem("o_read")
        root_asked, rooted, normed = sem("root_asked"), sem("rooted"), sem("normed")
        tr_done, tile_hi_done, tile_done = sem("tr_done"), sem("tile_hi_done"), sem("tile_done")
        x_stored = sem("x_stored")
        xt_stored = [sem("xt_stored0"), sem("xt_stored1")]
        dve_steps, held = sem("dve_steps"), sem("held")
        DVE_PER = NQ * 3 + NORM_STEPS

        block = ctx.enter_context(nc.Block())

        def every_b(eng, body):
            body(0)
            with eng.Fori(1, B) as b:
                body(b)

        Q_RUNS = [(0, 3, 0, True), (3, 2, 1, True), (5, 1, 2, False)]
        K_RUNS = [(0, 3, 0, False), (3, 2, 0, False), (5, 1, 0, False)]

        def load_stack(eng, b, q, runs, dst, src):
            v = src[b, q // 2].rearrange("c (d h) t -> c d (h t)", h=2 * QUAD)
            cols = slice(q % 2 * QUAD * T, (q % 2 + 1) * QUAD * T)
            for slot, n, plane, same in runs:
                if same:
                    planes_in = v[plane:plane + 1, :, cols].to_broadcast([n, D, QUAD * T])
                else:
                    planes_in = v[plane:plane + n, :, cols]
                eng.dma_start(dst[slot * D:(slot + n) * D, q % RING, :], planes_in).then_inc(stack_in[q % RING], 16)

        @block.sync
        def _(sp):
            def load_raw(b):
                sp.dma_start(xraw[:, :], xt_in[0][b].rearrange("p k t -> p (k t)")).then_inc(xraw_in, 16)

            if split_x:
                load_raw(0)
            for n in range(4):
                if n >= 2:
                    sp.wait_ge(w_done, n - 1)
                sp.dma_start(wraw[:, n % 2, :], wts[n].rearrange("p k c -> p (k c)")).then_inc(w_loaded[n % 2], 16)
                if n == 1:
                    sp.dma_start(cosr[:, :], cos_in).then_inc(const_in, 16)
                    sp.dma_start(sinr[:, :], sin_in).then_inc(const_in, 16)
                    sp.dma_start(ident[:, :], ident_in).then_inc(const_in, 16)
                    sp.dma_start(maskraw[:, :], mask_in).then_inc(const_in, 16)

            def store_rows(b):
                for t in range(TT):
                    sp.wait_ge(normed, TT * b + t + 1)
                    sp.dma_start(x_out[b, t * P:(t + 1) * P, :], y[:, t, :]).then_inc(x_stored, 16)

            def body(b, following):
                if not (isinstance(b, int) and b == 0):
                    store_rows(b - 1)

                def store_planes(m):
                    sp.wait_ge(plane_l, 8 * b + m + 1)
                    dst = (q_planes if m < 4 else k_planes)[b, m % 4]
                    sp.dma_start(dst.rearrange("c p t -> p c t"), planes(m)).then_inc(plane_out[m % RR], 16)

                def load(q, queries=True, keys=True):
                    at_least(sp, st_done, H * b + QUAD * max(q - RING + 1, 0))
                    hold(sp, held)
                    if q % 2 == 0 or q < RING:
                        sp.wait_ge(plane_out[q // 2], 32 * b + (32 if keys else 16))
                        hold(sp, held)
                    if queries:
                        load_stack(sp, b, q, Q_RUNS, qs, q_planes)
                    if keys:
                        load_stack(sp, b, q, K_RUNS, ks, k_planes)

                def maxima(q):
                    for i in range(3):
                        sp.wait_ge(max_split, 3 * (NQ * b + q) + i + 1)
                        sp.dma_start(qs[ROWS + i:ROWS + i + 1, q % RING, :].rearrange("p (m t) -> p m t", t=P),
                                     mplane[:, i, :]).then_inc(max_in[q % 2], 16)

                for m in range(8):
                    store_planes(m)
                    if m % 2:
                        for q in (m - 1, m) if m < 4 else (m - 5, m - 4):
                            load(q, queries=m < 4, keys=m >= 4)
                if split_x and following is not None:
                    sp.wait_ge(x_split, b + 1)
                    hold(sp, held)
                    at_least(sp, o_read, TT * b)
                    hold(sp, held)
                    load_raw(following)
                maxima(0)
                maxima(1)
                if isinstance(b, int) and b == 0:
                    sp.wait_ge(w_done, 4)
                at_least(sp, x_stored, 16 * TT * b)
                hold(sp, held)
                at_least(sp, tr_done, TT * b)
                hold(sp, held)
                sp.dma_start(y[:, :, :], x_in[b].rearrange("(t p) c -> p t c", p=P)).then_inc(res_in, 16)
                for q in range(RING, NQ):
                    load(q)
                    maxima(q - 2)
                maxima(NQ - 2)
                maxima(NQ - 1)

            body(0, 1)
            with sp.Fori(1, B - 1) as b:
                body(b, b + 1)
            body(B - 1, None)
            store_rows(B - 1)
            sp.wait_ge(x_stored, 16 * TT * B)
            sp.wait_ge(xt_stored[0], 16 * TT * B)
            sp.wait_ge(xt_stored[1], 16 * TT * B)

        @block.gpsimd
        def _(pool):
            pool.memset(vaug[:, :, :, D:D + 1], 1.0).then_inc(ones_set, 1)
            pool.wait_ge(ones_set, 1)
            pool.memset(ks[ROWS:P, :, :], 1.0).then_inc(ones_set, 1)
            pool.wait_ge(ones_set, 2)

            def load(b):
                for half, dst in zip(xt_in, (x_hi, x_lo)):
                    pool.dma_start(dst[:, :, :], half[b]).then_inc(x_loaded, 16)

            if not split_x:
                load(0)

            def body(b, following):
                for m in range(9):
                    if m < 8:
                        pool.wait_ge(rope_read, 24 * b + 3 * m + 3)
                        pool.tensor_tensor(rope_a(m), rope_a(m), rope_b(m), ALU.add).then_inc(rope_sum, 1)
                    if m >= 1:
                        pool.wait_ge(plane_h, 8 * b + m)
                        pool.tensor_tensor(rope_a(m - 1), rope_a(m - 1), planes(m - 1, 0), ALU.subtract).then_inc(rest_h, 1)
                for h in range(LAST):
                    if h % QUAD == 0 and QUAD <= h <= H:
                        k = h // QUAD - 1
                        pool.wait_ge(maxt_read, NQ * b + k + 1)
                        if k >= 1:
                            pool.wait_ge(max_in[(k - 1) % 2], 48 * (NQ // 2 * b + (k - 1) // 2 + 1))
                        hold(pool, held)
                        pool.tensor_copy(mplane[:, 0, :], mrest[:, :]).then_inc(max_split, 1)
                        pool.wait_ge(max_split, 3 * (NQ * b + k) + 1)
                        pool.tensor_tensor(mrest[:, :], mrest[:, :], mplane[:, 0, :], ALU.subtract).then_inc(max_step, 1)
                        pool.wait_ge(max_step, NQ * b + k + 1)
                        hold(pool, held)
                        pool.tensor_copy(mplane[:, 1, :], mrest[:, :]).then_inc(max_split, 1)
                        pool.wait_ge(max_split, 3 * (NQ * b + k) + 2)
                        pool.tensor_tensor(mplane[:, 2, :], mrest[:, :], mplane[:, 1, :],
                                           ALU.subtract).then_inc(max_split, 1)
                    if h == QUAD and following is not None:
                        pool.wait_ge(proj_done, 12 * b + 12)
                        hold(pool, held)
                        load(following)
                    if h == 2 * QUAD and split_x and following is not None:
                        pool.wait_ge(x_loaded, 16 * b + 16)
                        pool.wait_ge(xraw_in, 16 * b + 32)
                        pool.tensor_tensor(flat(x_lo), xraw[:, :], flat(x_hi).bitcast(F32), ALU.subtract).then_inc(x_split, 1)
                        pool.wait_ge(x_split, b + 2)
                    n = h - LAG
                    if n % QUAD == QUAD - 1 and QUAD <= n < H + QUAD:
                        q = n // QUAD - 1
                        pool.wait_ge(rec_done, NQ * b + q + 1)
                        at_least(pool, at_ready, NQ // 2 * b + q // 2)
                        pool.tensor_tensor(un[:, :, q % 2 * D:(q % 2 + 1) * D],
                                           u[:, q % 2, :].rearrange("p (n c) -> p n c", c=32)[:, :, 0:D],
                                           rec[:, q % 2, :].unsqueeze(2).to_broadcast([P, 16, D]),
                                           ALU.mult).then_inc(un_done, 1)
                    if n % 8 == 7 and n >= 15 or n == H + QUAD + 2:
                        g = min(n // 8 - 1, NQ // 2 - 1)
                        pool.wait_ge(at_hi_done, NQ // 2 * b + g + 1)
                        pool.tensor_tensor(at_lo[:, g, :], at[:, :], at_hi[:, g, :].bitcast(F32),
                                           ALU.subtract).then_inc(at_lo_done, 1)

            body(0, 1)
            with pool.Fori(1, B - 1) as b:
                body(b, b + 1)
            body(B - 1, None)

        @block.scalar
        def _(act):
            if split_x:
                act.wait_ge(xraw_in, 16)
                act.activation(flat(x_hi), xraw[:, :], ACT.Copy).then_inc(x_hi_done, 1)
            for n in range(4):
                act.wait_ge(w_loaded[n % 2], 16 * (n // 2 + 1))
                act.activation(flat(w_hi[n]), wraw[:, n % 2, :], ACT.Copy).then_inc(w_hi_done, 1)

            def copy_tiles(b):
                for t in range(TT):
                    act.wait_ge(tr_done, TT * b + t + 1)
                    at_least(act, xt_stored[t % 2], 64 * b + 32 * (t // 2))
                    act.activation(tile_hi[:, t % 2, :, :], bank(4 + t % 2).rearrange("p (k t) -> p k t", k=KT),
                                   ACT.Copy).then_inc(tile_hi_done, 1)
                    act.wait_ge(tile_done, TT * b + t + 1)
                    for half, tile in enumerate((tile_hi, tile_lo)):
                        act.dma_start(xt_out[half][b, :, :, t * P:(t + 1) * P],
                                      tile[:, t % 2, :, :].bitcast(F32)).then_inc(xt_stored[t % 2], 16)

            def body(b):
                for m in range(9):
                    if m < 8:
                        act.wait_ge(rope_sum, 8 * b + m + 1)
                        at_least(act, plane_out[m % RR], 32 * b + 16 * (m // RR))
                        act.activation(planes(m, 0), rope_a(m), ACT.Copy).then_inc(plane_h, 1)
                    if m >= 1:
                        act.wait_ge(rest_h, 8 * b + m)
                        act.activation(planes(m - 1, 1), rope_a(m - 1), ACT.Copy).then_inc(plane_m, 1)
                act.wait_ge(ones_set, 2)
                for t in range(TT):
                    act.wait_ge(proj_done, 12 * b + 8 + t + 1)
                    act.activation(vaug[:, t, :, 0:D], v_bank(t).rearrange("p (h d) -> p h d", d=D),
                                   ACT.Copy).then_inc(v_copied, 1)
                if not (isinstance(b, int) and b == 0):
                    copy_tiles(b - 1)

                def split_at(g):
                    act.wait_ge(at_ready, NQ // 2 * b + g + 1)
                    act.activation(at_hi[:, g, :], at[:, :], ACT.Copy).then_inc(at_hi_done, 1)

                for i in range(RR):
                    act.wait_ge(plane_out[i], 32 * b + 32)
                for h in range(H):
                    act.wait_ge(st_done, H * b + h + 1)
                    if h >= PTR:
                        act.wait_ge(pv_done, NQ * b + (h - PTR) // QUAD + 1)
                    act.activation(pt[:, h % PTR, :], ps[1][:, 0:SC], ACT.Exp,
                                   scale=float(D) ** -0.5).then_inc(exp_done, 1)
                    if h % 8 == 6 and h > 8:
                        split_at(h // 8 - 1)
                split_at(NQ // 2 - 1)
                act.wait_ge(root_asked, b + 1)
                act.activation(small[:, 1, :], small[:, 0, :], ACT.Sqrt).then_inc(rooted, 1)

            every_b(act, body)
            copy_tiles(B - 1)

        @block.vector
        def _(dve):
            dve.memset(pv[:, :], 0.0).then_inc(consts, 1)

            if split_x:
                dve.wait_ge(x_hi_done, 1)
                dve.tensor_tensor(flat(x_lo), xraw[:, :], flat(x_hi).bitcast(F32), ALU.subtract).then_inc(x_split, 1)
            for n in range(4):
                dve.wait_ge(w_hi_done, n + 1)
                dve.tensor_tensor(flat(w_lo[n]), wraw[:, n % 2, :], flat(w_hi[n]).bitcast(F32),
                                  ALU.subtract).then_inc(w_done, 1)
            dve.wait_ge(const_in, 64)
            dve.tensor_copy(identb[:, :], ident[:, :]).then_inc(consts, 1)
            dve.tensor_copy(flat(masks), maskraw[:, :]).then_inc(consts, 1)
            dve.wait_ge(consts, 3)

            def split_tile(b, t):
                dve.wait_ge(tile_hi_done, TT * b + t + 1)
                dve.tensor_tensor(tile_lo[:, t % 2, :, :], bank(4 + t % 2).rearrange("p (k t) -> p k t", k=KT),
                                  tile_hi[:, t % 2, :, :].bitcast(F32), ALU.subtract).then_inc(tile_done, 1)

            def body(b):
                st = Steps(dve, dve_steps, b * DVE_PER, DVE_PER)
                for m in range(10):
                    if m < 8:
                        src, c = bank(m % 6), rope_b(m)
                        dve.wait_ge(proj_done, 12 * b + m + 1)
                        at_least(dve, rope_sum, 8 * b + max(m - 1, 0))
                        at_least(dve, plane_l, 8 * b + max(m - RR + 1, 0))
                        dve.tensor_tensor(rope_a(m), src, cosr[:, :], ALU.mult).then_inc(rope_read, 1)
                        dve.tensor_tensor(c[0:64, :], src[64:P, :], sinr[0:64, :], ALU.mult).then_inc(rope_read, 1)
                        dve.tensor_tensor(c[64:P, :], src[0:64, :], sinr[64:P, :], ALU.mult).then_inc(rope_read, 1)
                    if m >= 2:
                        dve.wait_ge(plane_m, 8 * b + m - 1)
                        dve.tensor_tensor(planes(m - 2, 2), rope_a(m - 2), planes(m - 2, 1),
                                          ALU.subtract).then_inc(plane_l, 1)

                def by_token(q):
                    o = q % 2
                    dve.wait_ge(pv_done, NQ * b + q + 1)
                    at_least(dve, un_done, NQ * b + max(q - 1, 0))
                    dve.transpose(u[:, o, :], pv[:, o * NB:(o + 1) * NB]).then_inc(pv_read, 1)
                    dve.wait_ge(pv_read, NQ * b + q + 1)
                    dve.reciprocal(rec[:, o, :], u[:, o, D:T:32]).then_inc(rec_done, 1)

                def by_channel(q):
                    dve.wait_ge(un_done, NQ * b + q + 1)
                    at_least(dve, at_lo_done, NQ // 2 * b + q // 2)
                    dve.transpose(at[:, :], flat(un)).then_inc(at_ready, 1)

                for h in range(LAST):
                    if h < H:
                        if h % QUAD == 0:
                            at_least(dve, qmax_done, NQ * b + h // QUAD)
                        for i, (first, n, c0) in enumerate(((8, 2, 2 * NB), (0, 4, 0), (4, 4, NB))):
                            dve.wait_ge(s_done, 3 * (H * b + h) + i + 1)
                            dve.tensor_reduce(bmax[:, h % QUAD, first:first + n],
                                              ps[0][:, c0:c0 + n * P].rearrange("p (a k) -> p a k", k=P),
                                              AX.X, ALU.max).then_inc(s_read, 1)
                    if h - 1 in TR_AT and not (isinstance(b, int) and b == 0):
                        split_tile(b - 1, TR_AT.index(h - 1))
                    q = h // QUAD
                    if h % QUAD == QUAD - 1 and h < H:
                        dve.wait_ge(s_read, 3 * (H * b + h) + 3)
                        at_least(dve, maxt_done, NQ * b + q)
                        for i, (first, n) in enumerate(((7, 1), (8, 2), (4, 3), (0, 4))):
                            if i == 3:
                                st.wait()
                            ins = dve.tensor_reduce(qmax[:, :, i], bmax[:, :, first:first + n], AX.X, ALU.max)
                            if i == 3:
                                ins.then_inc(qmax_done, 1)
                            else:
                                st.inc(ins)
                    if h % QUAD == 0 and QUAD <= h <= H:
                        dve.wait_ge(maxt_done, NQ * b + q)
                        at_least(dve, max_split, 3 * (NQ * b + q - 1))
                        dve.tensor_scalar(mrest[:, :], maxt, -1.0, None, ALU.mult).then_inc(maxt_read, 1)
                    n = h - LAG
                    k = n // QUAD - 1
                    if n % QUAD == QUAD - 1 and 0 <= k < NQ:
                        by_token(k)
                    if n % QUAD == 2 and k % 2 == 0 and 0 < k <= NQ:
                        by_channel(k - 1)
                dve.wait_ge(res_in, 16 * b + 16)
                for t in range(TT):
                    dve.wait_ge(o_done, TT * b + t + 1)
                    dve.tensor_tensor(y[:, t, :], bank(t), y[:, t, :], ALU.add).then_inc(o_read, 1)
                dve.wait_ge(o_read, TT * b + TT)
                norm_rows(dve, st, y, stats, mv, small, root_asked, rooted, normed, b)
                st.end()

            every_b(dve, body)
            for t in range(TT):
                split_tile(B - 1, t)

        @block.tensor
        def _(pe):

            def w(n, k, cols):
                return w_hi[n][:, k, cols], w_lo[n][:, k, cols]

            def x(k, cols):
                return x_hi[:, k, cols], x_lo[:, k, cols]

            def transposes(b, t):
                pe.wait_ge(normed, TT * b + TT)
                at_least(pe, tile_done, TT * b + max(t - 1, 0))
                for k in range(KT):
                    last = pe.transpose(bank(4 + t % 2)[:, k * P:(k + 1) * P], y[:, t, k * P:(k + 1) * P], ident[:, :])
                last.then_inc(tr_done, 1)

            def body(b):
                every = slice(0, T)
                if split_x:
                    pe.wait_ge(x_split, b + 1)
                else:
                    pe.wait_ge(x_loaded, 32 * b + 32)
                for m in range(8):
                    if m < TT:
                        at_least(pe, o_read, TT * b)
                    if m >= 6:
                        pe.wait_ge(rope_read, 24 * b + 3 * (m - 5))
                    if m % 4 == 0:
                        pe.wait_ge(w_done, m // 4 + 1)
                    cols = slice(m % 4 * P, (m % 4 + 1) * P)
                    for k in range(KT):
                        last = product3(pe, bank(m % 6), w(m // 4, k, cols), x(k, every), k == 0, k == KT - 1)
                    last.then_inc(proj_done, 1)

                def project_values(t):
                    if t == 0:
                        pe.wait_ge(w_done, 3)
                    pe.wait_ge(rope_read, 24 * b + 3 * min(t + 4, 6))
                    for k in range(KT):
                        last = product3(pe, v_bank(t), x(k, slice(t * P, (t + 1) * P)), w(2, k, every), k == 0, k == KT - 1)
                    last.then_inc(proj_done, 1)

                for t in range(TT):
                    project_values(t)
                pe.wait_ge(rope_read, 24 * b + 24)
                pe.wait_ge(v_copied, TT * b + TT)
                if isinstance(b, int) and b == 0:
                    pe.wait_ge(consts, 3)

                def scores(h):
                    q, c0 = h // QUAD, h % QUAD * T
                    if h % QUAD == 0:
                        pe.wait_ge(stack_in[q % RING], 16 * len(Q_RUNS + K_RUNS) * (NQ // RING * b + q // RING + 1))

                    def one(i, start):
                        return pe.matmul(ps[0][:, S_AT[i]:S_AT[i] + P * (i + 1)],
                                         qs[0:ROWS, q % RING, c0 + i * P:c0 + (i + 1) * P],
                                         ks[0:ROWS, q % RING, c0:c0 + P * (i + 1)],
                                         start=start, stop=False, skip_group_check=True)

                    def mask(a, n):
                        return pe.matmul(ps[0][:, a:a + n], identb[:, :], masks[:, 0, 0:n],
                                         start=False, stop=True, skip_group_check=True)

                    def bank_read(i):
                        if h >= 1:
                            pe.wait_ge(s_read, 3 * (H * b + h - 1) + i + 1)

                    bank_read(0)
                    if h % QUAD == 1 and h > 1:
                        pe.wait_ge(maxt_read, NQ * b + h // QUAD)
                    one(1, True)
                    mask(1152, P).then_inc(s_done, 1)
                    bank_read(1)
                    one(3, True)
                    mask(384, P).then_inc(s_done, 1)
                    bank_read(2)
                    one(2, True)
                    one(0, False)
                    mask(768, 2 * P).then_inc(s_done, 1)

                def scores_t(h):
                    q, c0 = h // QUAD, h % QUAD * T
                    if h % QUAD == 0:
                        pe.wait_ge(max_in[q % 2], 48 * (NQ // 2 * b + q // 2 + 1))
                    at_least(pe, exp_done, H * b + h)
                    if h == 0:
                        at_least(pe, tile_done, TT * b)
                    rows = ROWS + 3

                    def one(j, start):
                        return pe.matmul(ps[1][:, ST_AT[j]:ST_AT[j] + T - P * j],
                                         ks[0:rows, q % RING, c0 + j * P:c0 + (j + 1) * P],
                                         qs[0:rows, q % RING, c0 + P * j:c0 + T],
                                         start=start, stop=False, skip_group_check=True)

                    def mask(a, n):
                        return pe.matmul(ps[1][:, a:a + n], identb[:, :], masks[:, 1, 0:n],
                                         start=False, stop=True, skip_group_check=True)

                    one(0, True)
                    mask(0, P)
                    one(3, True)
                    one(1, False)
                    mask(512, 2 * P)
                    one(2, True)
                    mask(1024, P).then_inc(st_done, 1)

                def values(q, js):
                    c = q % 2 * NB
                    if js[0] == 0:
                        pe.wait_ge(exp_done, H * b + QUAD * (q + 1))
                        if q >= 2:
                            pe.wait_ge(pv_read, NQ * b + q - 1)
                    for j in js:
                        for g in range(QUAD):
                            h = QUAD * q + g
                            last = pe.matmul(pv[32 * g:32 * g + D + 1, c + j * P:c + T], vaug[:, j, h, :],
                                             pt[:, h % PTR, ST_AT[j]:ST_AT[j] + T - P * j],
                                             start=j == 0, stop=j == TT - 1)
                    if js[-1] == TT - 1:
                        last.then_inc(pv_done, 1)

                def project_out(groups, tiles):
                    if groups[0] == 0:
                        pe.wait_ge(w_done, 4)
                        pe.wait_ge(s_read, 3 * H * (b + 1))
                        pe.wait_ge(maxt_read, NQ * (b + 1))
                    if TT - 1 in tiles:
                        pe.wait_ge(exp_done, H * (b + 1))
                    for g in groups:
                        pe.wait_ge(at_lo_done, NQ // 2 * b + g + 1)
                        for t in tiles:
                            cols = slice(t * P, (t + 1) * P)
                            last = product3(pe, bank(t), (at_hi[:, g, cols], at_lo[:, g, cols]), w(3, g, every),
                                            g == 0, g == NQ // 2 - 1)
                            if g == NQ // 2 - 1:
                                last.then_inc(o_done, 1)

                for h in range(LAST):
                    if h < H:
                        scores(h)
                    if h in TR_AT and not (isinstance(b, int) and b == 0):
                        transposes(b - 1, TR_AT.index(h))
                    n = h - LAG
                    if 0 <= n < H:
                        scores_t(n)
                    if h % QUAD == 0 and QUAD <= h <= H:
                        pe.wait_ge(qmax_done, NQ * b + h // QUAD)
                        pe.wait_ge(s_read, 3 * (H * b + min(h, H - 1)) + 1)
                        pe.transpose(maxt, qmax[:, :, :].rearrange("p h i -> p (h i)"), ident[:, :]).then_inc(maxt_done, 1)
                    if H < h <= H + 2:
                        project_out((h - H - 1,), range(3))
                    if QUAD <= n < H + QUAD and n % QUAD < 3:
                        values(n // QUAD - 1, ((0,), (1,), (2, 3))[n % QUAD])
                project_out(range(2), range(3, TT))
                project_out(range(2, NQ // 2), range(TT))

            every_b(pe, body)
            for t in range(TT):
                transposes(B - 1, t)


GT = 2
GROUPS = FT // GT


def gated_ffn_phase(nc, tag, x_in, xt_in, pairs, ident_in, x_out, xt_out, nf4_in, nf4_out):
    HALF = P // 2
    with ExitStack() as ctx:
        def sb(name, shape, dt=F32, at=ctx):
            return at.enter_context(nc.sbuf_tensor(f"{tag}_{name}", shape, dt))

        def sem(name):
            return nc.alloc_semaphore(f"{tag}_{name}")

        with ExitStack() as early:
            wd = [sb(f"w{n}_diff", s, at=early) for n, s in enumerate(([P, KT, F], [P, KT, F], [P, FT, C]))]
            wb = [sb(f"w{n}_base", s, at=early) for n, s in enumerate(([P, KT, F], [P, KT, F], [P, FT, C]))]
        w_hi = [sb(f"w{n}_hi", s, F32R) for n, s in enumerate(([P, KT, F], [P, KT, F], [P, FT, C]))]
        w_lo = [sb(f"w{n}_lo", s, F32R) for n, s in enumerate(([P, KT, F], [P, KT, F], [P, FT, C]))]
        x_hi = sb("x_hi", [P, KT, T], F32R)
        x_lo = sb("x_lo", [P, KT, T], F32R)
        with ExitStack() as early:
            made = sb("made", [P, 2, GT * C], at=early)
        y = sb("y", [P, TT, T])
        gate = sb("gate", [P, 2, T])
        h_hi = sb("h_hi", [P, 2, T], F32R)
        h_lo = sb("h_lo", [P, 2, T], F32R)
        sums = sb("sums", [P, 3, GROUPS])
        total = sb("total", [P, 3])
        coeff = sb("coeff", [P, 3])
        ident = sb("ident", [P, P])
        stats = sb("stats", [P, TT, 6])
        mv = sb("mv", [P, TT, 2])
        small = sb("small", [P, 4, TT])
        idx = sb("idx", [P, P], I32)
        scale = sb("scale", [P, P])
        code = sb("code", [P, 2, P])
        nw = sb("nw", [P, P])
        nw_hi = sb("nw_hi", [P, P], F32R)
        ps = ctx.enter_context(nc.psum_tensor(f"{tag}_ps", [P, 8, NB], F32))

        raw_in = [sem(f"raw_in{g}") for g in range(GROUPS)]
        diff_done, ones_set, ident_set = sem("diff_done"), sem("ones_set"), sem("ident_set")
        abs_done, sum_done, total_done, coeff_done = sem("abs_done"), sem("sum_done"), sem("total_done"), sem("coeff_done")
        sign_done, w_made, w_hi_done, w_done = sem("sign_done"), sem("w_made"), sem("w_hi_done"), sem("w_done")
        x_loaded = sem("x_loaded")
        up_done, silu_done, h_done, h_hi_done, h_lo_done, down_done = (
            sem("up_done"), sem("silu_done"), sem("h_done"), sem("h_hi_done"), sem("h_lo_done"), sem("down_done"))
        res_in, o_read = sem("res_in"), sem("o_read")
        root_asked, rooted, normed = sem("root_asked"), sem("rooted"), sem("normed")
        tr_done, tile_hi_done, tile_done, x_stored = sem("tr_done"), sem("tile_hi_done"), sem("tile_done"), sem("x_stored")
        xt_stored = [sem("xt_stored0"), sem("xt_stored1")]
        piece_in, nf4_step, nf4_stored = sem("piece_in"), sem("nf4_step"), sem("nf4_stored")
        held = sem("held")
        dve_steps = sem("dve_steps")
        block = ctx.enter_context(nc.Block())
        N = 3 * GROUPS

        def part(tensors, i):
            g, n = i // 3, i % 3
            if n == 2:
                return tensors[2][:, g * GT:(g + 1) * GT, :]
            return tensors[n][:, :, g * GT * P:(g + 1) * GT * P]

        def in_part(ap, i):
            return ap.rearrange("p (k n) -> p k n", k=GT if i % 3 == 2 else KT)

        def tile(half, t):
            return y[:, 2 * (t % 2) + half, :]

        def every_b(eng, body):
            body(0)
            with eng.Fori(1, B) as b:
                body(b)

        def first(b):
            return isinstance(b, int) and b == 0

        @block.sync
        def _(sp):
            for i in range(N):
                for s, dst in enumerate((wd, wb)):
                    sp.dma_start(part(dst, i), part([p[s] for p in pairs], i)).then_inc(raw_in[i // 3], 16)
            sp.dma_start(ident[:, :], ident_in).then_inc(ident_set, 16)

            def store_rows(b):
                for t in range(TT):
                    sp.wait_ge(normed, TT * b + t + 1)
                    sp.dma_start(x_out[b, t * P:(t + 1) * P, :], y[:, t, :]).then_inc(x_stored, 16)

            def store_tiles(b):
                for t in range(TT):
                    sp.wait_ge(tile_done, TT * b + t + 1)
                    for half in range(2):
                        sp.dma_start(xt_out[half][b, :, :, t * P:(t + 1) * P],
                                     tile(half, t).rearrange("p (k t) -> p k t", k=KT)).then_inc(xt_stored[t % 2], 16)

            def body(b):
                if first(b):
                    sp.wait_ge(w_done, N)
                else:
                    store_tiles(b - 1)
                    sp.wait_ge(xt_stored[0], 64 * b)
                    hold(sp, held)
                    sp.wait_ge(xt_stored[1], 64 * b)
                    hold(sp, held)
                sp.dma_start(y[:, :, :], x_in[b].rearrange("(t p) c -> p t c", p=P)).then_inc(res_in, 16)
                store_rows(b)

            every_b(sp, body)
            store_tiles(B - 1)
            sp.wait_ge(x_stored, 16 * TT * B)
            sp.wait_ge(xt_stored[0], 64 * B)
            sp.wait_ge(xt_stored[1], 64 * B)

        @block.gpsimd
        def _(pool):
            i_parts = nf4_in[0].rearrange("p k (g n) -> (k g) p n", n=P)
            s_parts = nf4_in[1].rearrange("h k (g n) -> (k g) h n", n=P)
            o_parts = [o.rearrange("p k (g n) -> (k g) p n", n=P) for o in nf4_out]
            STEPS = 2 * len(NF4) + 2
            PIECES = KT * C // P // B

            def load(b):
                for half, dst in enumerate((x_hi, x_lo)):
                    pool.dma_start(dst[:, :, :], xt_in[half][b]).then_inc(x_loaded, 16)

            def piece(c):
                st = Steps(pool, nf4_step, c * STEPS, STEPS)
                at_least(pool, nf4_step, STEPS * c)
                hold(pool, held)
                pool.dma_start(idx[:, :], i_parts[c]).then_inc(piece_in, 16)
                for half in range(2):
                    pool.dma_start(scale[half * HALF:(half + 1) * HALF, :],
                                   s_parts[c, half:half + 1].to_broadcast([HALF, P])).then_inc(piece_in, 16)
                pool.wait_ge(piece_in, 48 * c + 48)
                at_least(pool, nf4_stored, 32 * c)
                hold(pool, held)
                st.inc(pool.tensor_scalar(nw[:, :], idx[:, :], 0.0, NF4[0], ALU.is_equal, ALU.mult))
                for n, value in enumerate(NF4):
                    if n:
                        st.inc(pool.tensor_scalar(code[:, n % 2, :], idx[:, :], float(n), value, ALU.is_equal, ALU.mult))
                        st.wait()
                        st.inc(pool.tensor_tensor(nw[:, :], nw[:, :], code[:, n % 2, :], ALU.add))
                st.wait()
                st.done(pool.tensor_tensor(nw[:, :], nw[:, :], scale[:, :], ALU.mult))
                hold(pool, held)
                st.done(pool.tensor_copy(nw_hi[:, :], nw[:, :]))
                st.done(pool.tensor_tensor(code[:, 0, :], nw[:, :], nw_hi[:, :].bitcast(F32), ALU.subtract))
                st.end()
                hold(pool, held)
                pool.dma_start(o_parts[0][c], nw_hi[:, :].bitcast(F32)).then_inc(nf4_stored, 16)
                pool.dma_start(o_parts[1][c], code[:, 0, :]).then_inc(nf4_stored, 16)

            def body(b, following):
                for c in range(PIECES):
                    piece(PIECES * b + c)
                if following is not None:
                    pool.wait_ge(up_done, 2 * FT * (b + 1))
                    hold(pool, held)
                    load(following)

            load(0)
            body(0, 1)
            with pool.Fori(1, B - 1) as b:
                body(b, b + 1)
            body(B - 1, None)
            pool.wait_ge(nf4_stored, 32 * KT * C // P)

        @block.scalar
        def _(act):
            for i in range(N):
                act.wait_ge(diff_done, i + 1)
                if i >= 2:
                    act.wait_ge(abs_done, i - 1)
                junk = ps[:, 2 * (i % 2):2 * (i % 2) + 2, :].rearrange("p a n -> p (a n)")
                act.activation(in_part(junk, i), part(wd, i), ACT.Abs,
                               accum_out=sums[:, i % 3, i // 3:i // 3 + 1]).then_inc(abs_done, 1)

            def make(g):
                for i in range(3 * g, 3 * g + 3):
                    if g == 0:
                        act.wait_ge(abs_done, N)
                    act.activation(part(wd, i), part(wd, i), ACT.Sign).then_inc(sign_done, 1)
                for i in range(3 * g, 3 * g + 3):
                    act.wait_ge(w_made, i + 1)
                    act.activation(part(w_hi, i), in_part(made[:, i % 2, :], i), ACT.Copy).then_inc(w_hi_done, 1)

            def copy_tiles(b):
                for t in range(TT):
                    act.wait_ge(tr_done, TT * b + TT)
                    if t < 2:
                        act.wait_ge(x_stored, 16 * TT * (b + 1))
                    at_least(act, xt_stored[t % 2], 64 * b + 32 * (t // 2))
                    act.activation(tile(0, t).bitcast(F32R), ps[:, t, :], ACT.Copy).then_inc(tile_hi_done, 1)

            make(0)
            make(1)

            def body(b):
                for f in range(FT):
                    n = FT * b + f
                    act.wait_ge(up_done, 2 * n + 1)
                    at_least(act, h_lo_done, max(f - 1, 0) + FT * b)
                    act.activation(gate[:, f % 2, :], ps[:, 4 + f % 2 * 2, :], ACT.Silu).then_inc(silu_done, 1)
                    act.wait_ge(h_done, n + 1)
                    at_least(act, down_done, FT * b + max(f - 1, 0))
                    act.activation(h_hi[:, f % 2, :], gate[:, f % 2, :], ACT.Copy).then_inc(h_hi_done, 1)
                    if f == 1 and not first(b):
                        copy_tiles(b - 1)
                    if first(b) and f % 2 == 0 and f // 2 + 2 < GROUPS:
                        make(f // 2 + 2)
                act.wait_ge(root_asked, b + 1)
                act.activation(small[:, 1, :], small[:, 0, :], ACT.Sqrt).then_inc(rooted, 1)

            every_b(act, body)
            copy_tiles(B - 1)

        DVE_PER = NORM_STEPS

        @block.vector
        def _(dve):
            dve.memset(y[:, 0, 0:P], 1.0).then_inc(ones_set, 1)
            for i in range(N):
                dve.wait_ge(raw_in[i // 3], 96)
                dve.tensor_tensor(part(wd, i), part(wd, i), part(wb, i),
                                  ALU.subtract).then_inc(diff_done, 1)
            dve.wait_ge(abs_done, N)
            dve.tensor_reduce(total[:, :], sums[:, :, :], AX.X, ALU.add).then_inc(sum_done, 1)
            dve.wait_ge(total_done, 1)
            dve.tensor_scalar(coeff[:, :], ps[:, 4, 0:3], 1.0 / (C * F), None, ALU.mult).then_inc(coeff_done, 1)
            dve.wait_ge(coeff_done, 1)

            def make(g):
                for i in range(3 * g, 3 * g + 4):
                    if i < 3 * g + 3:
                        dve.wait_ge(sign_done, i + 1)
                        if i >= 2:
                            dve.wait_ge(w_done, i - 1)
                        dve.scalar_tensor_tensor(out=in_part(made[:, i % 2, :], i), in0=part(wd, i),
                                                 scalar=coeff[:, i % 3:i % 3 + 1], in1=part(wb, i),
                                                 op0=ALU.mult, op1=ALU.add).then_inc(w_made, 1)
                    if i > 3 * g:
                        j = i - 1
                        dve.wait_ge(w_hi_done, j + 1)
                        dve.tensor_tensor(part(w_lo, j), in_part(made[:, j % 2, :], j), part(w_hi, j).bitcast(F32),
                                          ALU.subtract).then_inc(w_done, 1)

            make(0)
            make(1)

            def split_tiles(b):
                for t in range(TT):
                    dve.wait_ge(tile_hi_done, TT * b + t + 1)
                    dve.tensor_tensor(tile(1, t), ps[:, t, :], tile(0, t), ALU.subtract).then_inc(tile_done, 1)

            def body(b):
                st = Steps(dve, dve_steps, b * DVE_PER, DVE_PER)
                for f in range(FT):
                    n = FT * b + f
                    dve.wait_ge(silu_done, n + 1)
                    dve.wait_ge(up_done, 2 * n + 2)
                    dve.tensor_tensor(gate[:, f % 2, :], ps[:, 5 + f % 2 * 2, :], gate[:, f % 2, :], ALU.mult).then_inc(h_done, 1)
                    dve.wait_ge(h_hi_done, n + 1)
                    dve.tensor_tensor(h_lo[:, f % 2, :], gate[:, f % 2, :], h_hi[:, f % 2, :].bitcast(F32),
                                      ALU.subtract).then_inc(h_lo_done, 1)
                    if f == 1 and not first(b):
                        split_tiles(b - 1)
                    if first(b) and f % 2 == 0 and f // 2 + 2 < GROUPS:
                        make(f // 2 + 2)
                dve.wait_ge(res_in, 16 * b + 16)
                dve.wait_ge(down_done, FT * (b + 1))
                for t in range(TT):
                    dve.tensor_tensor(y[:, t, :], ps[:, t, :], y[:, t, :], ALU.add).then_inc(o_read, 1)
                    dve.wait_ge(o_read, TT * b + t + 1)
                norm_rows(dve, st, y, stats, mv, small, root_asked, rooted, normed, b)
                st.end()

            every_b(dve, body)
            split_tiles(B - 1)

        @block.tensor
        def _(pe):
            pe.wait_ge(ones_set, 1)
            pe.wait_ge(sum_done, 1)
            pe.matmul(ps[:, 4, 0:3], y[:, 0, 0:P], total[:, :], start=True, stop=True).then_inc(total_done, 1)
            pe.wait_ge(coeff_done, 1)
            pe.wait_ge(ident_set, 16)

            def transposes(b):
                for t in range(TT):
                    pe.wait_ge(normed, TT * b + t + 1)
                    for k in range(KT):
                        last = pe.transpose(ps[:, t, k * P:(k + 1) * P], y[:, t, k * P:(k + 1) * P], ident[:, :])
                    last.then_inc(tr_done, 1)

            def body(b):
                def up(f):
                    if first(b):
                        pe.wait_ge(w_done, 3 * (f // GT) + 2)
                    if f >= 2:
                        pe.wait_ge(h_done, FT * b + f - 1)
                    else:
                        at_least(pe, h_done, FT * b)
                    cols = slice(f * P, (f + 1) * P)
                    for m in range(2):
                        for k in range(KT):
                            last = product3(pe, ps[:, 4 + f % 2 * 2 + m, :], (w_hi[m][:, k, cols], w_lo[m][:, k, cols]),
                                            (x_hi[:, k, :], x_lo[:, k, :]), k == 0, k == KT - 1)
                        last.then_inc(up_done, 1)

                def down(f):
                    if first(b):
                        pe.wait_ge(w_done, 3 * (f // GT) + 3)
                    pe.wait_ge(h_lo_done, FT * b + f + 1)
                    for t in range(TT):
                        cols = slice(t * P, (t + 1) * P)
                        last = product3(pe, ps[:, t, :], (h_hi[:, f % 2, cols], h_lo[:, f % 2, cols]),
                                        (w_hi[2][:, f, :], w_lo[2][:, f, :]), f == 0, f == FT - 1)
                    last.then_inc(down_done, 1)

                pe.wait_ge(x_loaded, 32 * b + 32)
                up(0)
                up(1)
                if not first(b):
                    transposes(b - 1)
                for f in range(2, FT):
                    up(f)
                    if f == 2:
                        at_least(pe, tile_done, TT * b)
                    down(f - 2)
                down(FT - 2)
                down(FT - 1)

            every_b(pe, body)
            transposes(B - 1)


def quantised_ffn_phase(nc, tag, x_in, xt_in, w_in_halves, bias, out):
    with ExitStack() as ctx:
        def sb(name, shape, dt=F32):
            return ctx.enter_context(nc.sbuf_tensor(f"{tag}_{name}", shape, dt))

        def sem(name):
            return nc.alloc_semaphore(f"{tag}_{name}")

        w_hi = sb("w_hi", [P, KT, C], F32R)
        w_lo = sb("w_lo", [P, KT, C], F32R)
        biasr = sb("biasr", [P, C])
        x_hi = sb("x_hi", [P, 2, KT, T], F32R)
        x_lo = sb("x_lo", [P, 2, KT, T], F32R)
        y = sb("y", [P, 2, TT, T])
        stats = sb("stats", [P, TT, 6])
        mv = sb("mv", [P, TT, 2])
        small = sb("small", [P, 4, TT])
        ps = ctx.enter_context(nc.psum_tensor(f"{tag}_ps", [P, 8, NB], F32))

        w_loaded, bias_in, x_loaded = sem("w_loaded"), sem("bias_in"), [sem("x_loaded0"), sem("x_loaded1")]
        res_in, biased, o_done, o_read = [sem("res_in0"), sem("res_in1")], sem("biased"), sem("o_done"), sem("o_read")
        root_asked, rooted, normed = sem("root_asked"), sem("rooted"), sem("normed")
        stored, dve_steps = [sem("stored0"), sem("stored1")], sem("dve_steps")
        block = ctx.enter_context(nc.Block())

        @block.sync
        def _(sp):
            for b in range(B):
                i = b % 2
                if b == 0:
                    sp.dma_start(biasr[:, :], bias.to_broadcast([P, C])).then_inc(bias_in, 16)
                if b >= 2:
                    sp.wait_ge(stored[i], 16 * TT * (b // 2))
                sp.dma_start(y[:, i, :, :], x_in[b].rearrange("(t p) c -> p t c", p=P)).then_inc(res_in[i], 16)

        @block.gpsimd
        def _(pool):
            for half, dst in enumerate((w_hi, w_lo)):
                pool.dma_start(dst[:, :, :], w_in_halves[half]).then_inc(w_loaded, 16)

            def load(b):
                if b >= 2:
                    pool.wait_ge(o_done, TT * (b - 1))
                for half, dst in enumerate((x_hi, x_lo)):
                    pool.dma_start(dst[:, b % 2, :, :], xt_in[half][b]).then_inc(x_loaded[b % 2], 16)

            load(0)
            for b in range(B):
                if b + 1 < B:
                    load(b + 1)
                pool.wait_ge(bias_in, 16)
                pool.wait_ge(res_in[b % 2], 16 * (b // 2 + 1))
                for t in range(TT):
                    pool.tensor_tensor(y[:, b % 2, t, :], y[:, b % 2, t, :], biasr[:, :], ALU.add).then_inc(biased, 1)

        @block.scalar
        def _(act):
            for b in range(B):
                act.wait_ge(root_asked, b + 1)
                act.activation(small[:, 1, :], small[:, 0, :], ACT.Sqrt).then_inc(rooted, 1)
                for t in range(TT):
                    act.wait_ge(normed, TT * b + t + 1)
                    act.dma_start(out[b, t * P:(t + 1) * P, :], y[:, b % 2, t, :]).then_inc(stored[b % 2], 16)
            act.wait_ge(stored[0], 16 * TT * B // 2)
            act.wait_ge(stored[1], 16 * TT * B // 2)

        @block.vector
        def _(dve):
            for b in range(B):
                st = Steps(dve, dve_steps, b * NORM_STEPS, NORM_STEPS)
                dve.wait_ge(biased, TT * (b + 1))
                for t in range(TT):
                    dve.wait_ge(o_done, TT * b + t + 1)
                    dve.tensor_tensor(y[:, b % 2, t, :], ps[:, b % 2 * TT + t, :], y[:, b % 2, t, :], ALU.add).then_inc(o_read, 1)
                    dve.wait_ge(o_read, TT * b + t + 1)
                norm_rows(dve, st, y[:, b % 2, :, :], stats, mv, small, root_asked, rooted, normed, b)
                st.end()

        @block.tensor
        def _(pe):
            pe.wait_ge(w_loaded, 32)
            for b in range(B):
                pe.wait_ge(x_loaded[b % 2], 32 * (b // 2 + 1))
                if b >= 2:
                    pe.wait_ge(o_read, TT * (b - 1))
                for t in range(TT):
                    cols = slice(t * P, (t + 1) * P)
                    for k in range(KT):
                        last = product3(pe, ps[:, b % 2 * TT + t, :], (x_hi[:, b % 2, k, cols], x_lo[:, b % 2, k, cols]),
                                        (w_hi[:, k, :], w_lo[:, k, :]), k == 0, k == KT - 1)
                    last.then_inc(o_done, 1)


def head_channels(order):
    rows = []
    for tile in range(C // P):
        for d in range(D):
            half, i = d // (D // 2), d % (D // 2)
            within = 2 * i + half if order == "pairs" else half * (D // 2) + i
            rows += [(tile * 2 * QUAD + h) * D + within for h in range(2 * QUAD)]
    return np.array(rows)


def output_channels():
    return np.array([((2 * g + o) * QUAD + h) * D + d
                     for g in range(NQ // 2) for h in range(QUAD) for o in range(2) for d in range(D)])


def rotary(order):
    f = np.float32
    t = np.arange(T, dtype=f)
    if order == "pairs":
        freqs = np.ones(D // 2, f)
    else:
        freqs = (f(1.0) / np.power(f(10000.0), np.arange(0, D, 2, dtype=f) / f(D))).astype(f)
    theta = (t[None, :] * freqs[:, None]).astype(f).astype(np.float64)
    cos = np.repeat(np.concatenate([np.cos(theta)] * 2), 2 * QUAD, axis=0).astype(f)
    sin = np.repeat(np.concatenate([-np.sin(theta), np.sin(theta)]), 2 * QUAD, axis=0).astype(f)
    return cos, sin


def by_partition(w):
    k, n = w.shape
    return np.ascontiguousarray(w.reshape(k // P, P, n).transpose(1, 0, 2))


def causal_masks():
    later = np.triu(np.ones((P, P)), 1) * -1e30
    return np.concatenate([later, later, later.T, later.T], axis=1).astype(np.float32)


def two_layers(nc, x, xt, l0, ffn, l1, rope0, rope1, ident, masks, w_idx, absmax, bias, out):
    def rows(name):
        return nc.dram_tensor(name, [B, T, C], F32).ap()

    def channels(name):
        return nc.dram_tensor(name, [B, P, KT, T], F32).ap()

    q_planes = nc.dram_tensor("q_planes", [B, C // P, 3, P, T], BF16).ap()
    k_planes = nc.dram_tensor("k_planes", [B, C // P, 3, P, T], BF16).ap()
    def halves(name):
        return [channels(f"{name}_hi"), channels(f"{name}_lo")]

    x1, x2, x3 = rows("x1"), rows("x2"), rows("x3")
    x1t, x2t, x3t = halves("x1t"), halves("x2t"), halves("x3t")
    nf4 = [nc.dram_tensor(f"nf4_{half}", [P, KT, C], F32).ap() for half in ("hi", "lo")]
    with nc.cleanup_on_exit():
        attention_phase(nc, "a0", x, [xt], l0, *rope0, ident, masks, x1, x1t, q_planes, k_planes)
    with nc.cleanup_on_exit():
        gated_ffn_phase(nc, "f0", x1, x1t, ffn, ident, x2, x2t, (w_idx, absmax), nf4)
    with nc.cleanup_on_exit():
        attention_phase(nc, "a1", x2, x2t, l1, *rope1, ident, masks, x3, x3t, q_planes, k_planes)
    with nc.cleanup_on_exit():
        quantised_ffn_phase(nc, "f1", x3, x3t, nf4, bias, out)


def kernel(**inputs):
    import concourse.bacc as bacc
    from concourse.bass_utils import run_bass_kernel_spmd

    g = {n: np.asarray(a) for n, a in inputs.items()}
    x = g["L0_attn_x"]
    arrays = {
        "x": x,
        "xt": np.ascontiguousarray(x.transpose(0, 2, 1).reshape(B, KT, P, T).transpose(0, 2, 1, 3)),
    }
    for layer, order in ((0, "pairs"), (1, "halves")):
        ch = head_channels(order)
        for n in "qk":
            arrays[f"w{n}{layer}"] = by_partition(g[f"L{layer}_attn_w{n}"][ch].T)
        arrays[f"wv{layer}"] = by_partition(g[f"L{layer}_attn_wv"].T)
        arrays[f"wo{layer}"] = by_partition(g[f"L{layer}_attn_wo"].T[output_channels()])
        arrays[f"cos{layer}"], arrays[f"sin{layer}"] = rotary(order)
    for n in (1, 3, 2):
        arrays[f"w{n}"] = by_partition(g[f"L0_ffn_w{n}"].T)
        arrays[f"mean_w{n}"] = by_partition(g[f"L0_ffn_mean_w{n}"].T)
    arrays["ident"] = np.eye(P, dtype=np.float32)
    arrays["masks"] = causal_masks()
    arrays["w_idx"] = by_partition(g["L1_ffn_w_idx"].T)
    arrays["absmax"] = np.ascontiguousarray(g["L1_ffn_absmax"].reshape(C, KT, 2).transpose(2, 1, 0))
    arrays["bias"] = g["L1_ffn_bias"].reshape(1, C)

    nc = bacc.Bacc("TRN2", target_bir_lowering=False, num_devices=1)
    arrays = {f"in_{n}": np.ascontiguousarray(a) for n, a in arrays.items()}
    t = {n[3:]: nc.dram_tensor(n, a.shape, mybir.dt.from_np(a.dtype), kind="ExternalInput").ap()
         for n, a in arrays.items()}
    out = nc.dram_tensor("out", (B, T, C), F32, kind="ExternalOutput").ap()
    two_layers(nc, t["x"], t["xt"], [t[f"w{n}0"] for n in "qkvo"],
               [(t[f"w{n}"], t[f"mean_w{n}"]) for n in (1, 3, 2)], [t[f"w{n}1"] for n in "qkvo"],
               (t["cos0"], t["sin0"]), (t["cos1"], t["sin1"]), t["ident"], t["masks"],
               t["w_idx"], t["absmax"], t["bias"], out)
    r = run_bass_kernel_spmd(nc, [arrays], core_ids=[0])
    return r.results[0]["out"]
```

```python
from contextlib import ExitStack

import numpy as np

import concourse.bass as bass
from concourse import mybir

ALU = mybir.AluOpType
ACT = mybir.ActivationFunctionType
AX = mybir.AxisListType
F32 = mybir.dt.float32
F32R = mybir.dt.float32r
BF16 = mybir.dt.bfloat16
I32 = mybir.dt.int32

P = 128
B, T, C = 4, 512, 512
H = 32
D = C // H
KT = C // P
TT = T // P
F = 1792
FT = F // P
NB = 512
QUAD = 4
NQ = H // QUAD
RING = 4
PTR = 7
LAG = 7
LAST = H + LAG + QUAD + 3
TR_AT = (3, 3, 4, 5)
NSLOT = 6
ROWS = NSLOT * D
SC = T + 384 + 256 + 128
S_AT = {3: 0, 2: 512, 0: 896, 1: 1024}
ST_AT = {0: 0, 3: 512, 1: 640, 2: 1024}
EPS = 1e-5
BESIDE = 12
PIECE = 3 * KT * F // (BESIDE * B)
SLOTS = 3
NF4 = [-1.0, -0.6961928009986877, -0.5250730514526367, -0.39491748809814453, -0.28444138169288635,
       -0.18477343022823334, -0.09105003625154495, 0.0, 0.07958029955625534, 0.16093020141124725,
       0.24611230194568634, 0.33791524171829224, 0.44070982933044434, 0.5626170039176941,
       0.7229568362236023, 1.0]



class Steps:

    def __init__(self, eng, sem, base, per):
        self.eng, self.sem, self.base, self.per, self.n = eng, sem, base, per, 0

    def inc(self, ins):
        ins.then_inc(self.sem, 1)
        self.n += 1

    def wait(self):
        self.eng.wait_ge(self.sem, self.base + self.n)

    def done(self, ins):
        self.inc(ins)
        self.wait()

    def end(self):
        assert self.n == self.per, (self.n, self.per)


def product3(eng, out, lhs, rhs, start=True, stop=True):
    (lh, ll), (rh, rl) = lhs, rhs
    eng.matmul(out, lh, rh, start=start, stop=False)
    eng.matmul(out, lh, rl, start=False, stop=False)
    return eng.matmul(out, ll, rh, start=False, stop=stop)


def at_least(eng, sem, value):
    if not (isinstance(value, int) and value == 0):
        eng.wait_ge(sem, value)


def hold(eng, sem):
    eng.sem_inc(sem, 1)


NORM_STEPS = 2 * TT + 5


def norm_moments(dve, st, y, stats, mv, small, root_asked):
    for t in range(TT):
        st.inc(dve.bn_stats(stats[:, t, :], y[:, t, :]))
    st.wait()
    dve.memset(small[:, 2, :], 0.0)
    for t in range(TT):
        st.inc(dve.bn_aggr(mv[:, t, :], stats[:, t, :]))
    st.wait()
    dve.tensor_scalar(small[:, 0, :], mv[:, :, 1], EPS, None, ALU.add).then_inc(root_asked, 1)


def norm_scale(dve, st, small, root_asked, rooted, b):
    dve.wait_ge(rooted, b + 1)
    dve.wait_ge(root_asked, b + 1)
    v, s, r = small[:, 0, :], small[:, 1, :], small[:, 2, :]
    st.done(dve.reciprocal(r, s))
    st.done(dve.tensor_tensor(r, r, v, ALU.mult))
    st.done(dve.tensor_tensor(r, r, s, ALU.add))
    st.done(dve.tensor_scalar(r, r, 0.5, None, ALU.mult))
    st.done(dve.reciprocal(small[:, 3, :], r))
    st.end()


def norm_apply(dve, y, mv, small, normed):
    for t in range(TT):
        dve.tensor_scalar(y[:, t, :], y[:, t, :], mv[:, t, 0:1], small[:, 3, t:t + 1],
                          ALU.subtract, ALU.mult).then_inc(normed, 1)


def norm_rows(dve, st, y, stats, mv, small, root_asked, rooted, normed, b):
    norm_moments(dve, st, y, stats, mv, small, root_asked)
    norm_scale(dve, st, small, root_asked, rooted, b)
    norm_apply(dve, y, mv, small, normed)


def flat(ap):
    return ap[:, :, :].rearrange("p a b -> p (a b)")


def attention_phase(nc, tag, x_in, xt_in, wts, cos_in, sin_in, ident_in, mask_in, x_out, xt_out,
                    q_planes, k_planes, sums_of=None):
    split_x = len(xt_in) == 1
    with ExitStack() as ctx:
        def sb(name, shape, dt=F32, at=ctx):
            return at.enter_context(nc.sbuf_tensor(f"{tag}_{name}", shape, dt))

        def sem(name):
            return nc.alloc_semaphore(f"{tag}_{name}")

        w_hi = [sb(f"w{n}_hi", [P, KT, C], F32R) for n in "qkvo"]
        w_lo = [sb(f"w{n}_lo", [P, KT, C], F32R) for n in "qkvo"]
        x_hi = sb("x_hi", [P, KT, T], F32R)
        x_lo = sb("x_lo", [P, KT, T], F32R)
        vaug = sb("vaug", [P, TT, H, D + 1])
        cosr = sb("cosr", [P, T])
        sinr = sb("sinr", [P, T])
        qs = sb("qs", [P, RING, QUAD * T], BF16)
        ks = sb("ks", [P, RING, QUAD * T], BF16)
        u = sb("u", [P, 2, T])
        un = sb("un", [P, 16, 32])
        at = sb("at", [P, T])
        rec = sb("rec", [P, 2, 16])
        ident = sb("ident", [P, P])
        identb = sb("identb", [P, P], BF16)
        masks = sb("masks", [P, 2, 2 * P], BF16)
        bmax = sb("bmax", [P, QUAD, 10])
        qmax = sb("qmax", [P, QUAD, TT])
        mplane = sb("mplane", [QUAD * TT, 3, P], BF16)
        mrest = sb("mrest", [QUAD * TT, P])
        stats = sb("stats", [P, TT, 6])
        mv = sb("mv", [P, TT, 2])
        small = sb("small", [P, 4, TT])
        if sums_of:
            wpiece = sb("wpiece", [P, SLOTS, 2, PIECE])
            sums = sb("sums", [P, 2, BESIDE])
        with ExitStack() as early:
            xraw = sb("xraw", [P, KT * T], at=early)
            wraw = sb("wraw", [P, 2, KT * C], at=early)
        at_hi = sb("at_hi", [P, NQ // 2, T], F32R)
        at_lo = sb("at_lo", [P, NQ // 2, T], F32R)
        y = sb("y", [P, TT, T])
        pt = sb("pt", [P, PTR, SC])
        RR = 4

        def planes(m, i=None):
            v = pt[:, m % RR, 0:3 * T // 2].bitcast(BF16).rearrange("p (c t) -> p c t", c=3)
            return v if i is None else v[:, i, :]

        def rope_a(m):
            return pt[:, m % RR, 3 * T // 2:3 * T // 2 + T]

        def rope_b(m):
            return u[:, m % 2, :]

        ps = [ctx.enter_context(nc.psum_tensor(f"{tag}_ps{i}", [P, 3 * NB], F32)) for i in range(2)]
        pv = ctx.enter_context(nc.psum_tensor(f"{tag}_pv", [P, 2 * NB], F32))

        def bank(n):
            return ps[n // 3][:, (n % 3) * NB:(n % 3 + 1) * NB]

        def tiles(half):
            return (at_lo, at_hi)[half]

        def tr_bank(t):
            return bank((4, 5, 3, 4)[t])

        def v_bank(t):
            return bank((3, 4, 5, 3)[t])

        maxt = ps[0][0:QUAD * TT, SC:SC + P]

        w_loaded = [sem("w_loaded0"), sem("w_loaded1")]
        w_hi_done, w_done = sem("w_hi_done"), sem("w_done")
        trig_in, const_in, consts, ones_set = sem("trig_in"), sem("const_in"), sem("consts"), sem("ones_set")
        xraw_in, x_hi_done, x_split = sem("xraw_in"), sem("x_hi_done"), sem("x_split")
        x_loaded, proj_done, rope_read, v_copied = sem("x_loaded"), sem("proj_done"), sem("rope_read"), sem("v_copied")
        rope_sum, plane_h, rest_h, plane_m, plane_l = (
            sem("rope_sum"), sem("plane_h"), sem("rest_h"), sem("plane_m"), sem("plane_l"))
        plane_out = [sem(f"plane_out{i}") for i in range(RR)]
        stack_in = [sem(f"stack_in{r}") for r in range(RING)]
        s_done, s_read, qmax_done, maxt_done = sem("s_done"), sem("s_read"), sem("qmax_done"), sem("maxt_done")
        maxt_read, max_split, max_step = sem("maxt_read"), sem("max_split"), sem("max_step")
        max_in = [sem("max_in0"), sem("max_in1")]
        st_done, exp_done, pv_done, pv_read = sem("st_done"), sem("exp_done"), sem("pv_done"), sem("pv_read")
        rec_done, un_done = sem("rec_done"), sem("un_done")
        at_ready, at_hi_done, at_lo_done = sem("at_ready"), sem("at_hi_done"), sem("at_lo_done")
        res_in, o_done, o_read = sem("res_in"), sem("o_done"), sem("o_read")
        root_asked, rooted, normed = sem("root_asked"), sem("rooted"), sem("normed")
        tr_done, tile_hi_done, tile_done = sem("tr_done"), sem("tile_hi_done"), sem("tile_done")
        x_stored = sem("x_stored")
        xt_stored = sem("xt_stored")
        dve_steps, held = sem("dve_steps"), sem("held")
        piece_in, diff_done, abs_done, sums_added, sums_stored = (
            [sem(f"piece_in{i}") for i in range(SLOTS)], sem("diff_done"), sem("abs_done"), sem("sums_added"), sem("sums_stored"))
        norm_steps = sem("norm_steps")
        DVE_PER = NQ * 3

        block = ctx.enter_context(nc.Block())

        def every_b(eng, body):
            body(0)
            with eng.Fori(1, B) as b:
                body(b)

        Q_RUNS = [(0, 3, 0, True), (3, 2, 1, True), (5, 1, 2, False)]
        K_RUNS = [(0, 3, 0, False), (3, 2, 0, False), (5, 1, 0, False)]

        def load_stack(eng, b, q, runs, dst, src):
            v = src[b, q // 2].rearrange("c (d h) t -> c d (h t)", h=2 * QUAD)
            cols = slice(q % 2 * QUAD * T, (q % 2 + 1) * QUAD * T)
            for slot, n, plane, same in runs:
                if same:
                    planes_in = v[plane:plane + 1, :, cols].to_broadcast([n, D, QUAD * T])
                else:
                    planes_in = v[plane:plane + n, :, cols]
                eng.dma_start(dst[slot * D:(slot + n) * D, q % RING, :], planes_in).then_inc(stack_in[q % RING], 16)

        @block.sync
        def _(sp):
            def load_raw(b):
                sp.dma_start(xraw[:, :], xt_in[0][b].rearrange("p k t -> p (k t)")).then_inc(xraw_in, 16)

            if split_x:
                load_raw(0)
            for n in range(4):
                if n >= 2:
                    sp.wait_ge(w_done, n - 1)
                sp.dma_start(wraw[:, n % 2, :], wts[n].rearrange("p k c -> p (k c)")).then_inc(w_loaded[n % 2], 16)
                if n == 1:
                    sp.dma_start(cosr[:, :], cos_in).then_inc(trig_in, 16)
                    sp.dma_start(sinr[:, :], sin_in).then_inc(trig_in, 16)
            sp.dma_start(ident[:, :], ident_in).then_inc(const_in, 16)
            sp.dma_start(at[:, :], mask_in).then_inc(const_in, 16)

            def store_rows(b):
                for t in range(TT):
                    sp.wait_ge(normed, TT * b + t + 1)
                    sp.dma_start(x_out[b, t * P:(t + 1) * P, :], y[:, t, :]).then_inc(x_stored, 16)

            def store_tiles(b, ts):
                for t in ts:
                    sp.wait_ge(tile_done, TT * b + t + 1)
                    for half in range(2):
                        sp.dma_start(xt_out[half][b, :, :, t * P:(t + 1) * P],
                                     tiles(half)[:, t, :].rearrange("p (k t) -> p k t", k=KT).bitcast(F32)).then_inc(xt_stored, 16)

            def body(b, following):
                def store_planes(m):
                    sp.wait_ge(plane_l, 8 * b + m + 1)
                    dst = (q_planes if m < 4 else k_planes)[b, m % 4]
                    sp.dma_start(dst.rearrange("c p t -> p c t"), planes(m)).then_inc(plane_out[m % RR], 16)

                def load(q, queries=True, keys=True):
                    at_least(sp, st_done, H * b + QUAD * max(q - RING + 1, 0))
                    hold(sp, held)
                    if q % 2 == 0 or q < 2:
                        sp.wait_ge(plane_out[q // 2], 32 * b + (32 if keys else 16))
                        hold(sp, held)
                    if queries:
                        load_stack(sp, b, q, Q_RUNS, qs, q_planes)
                    if keys:
                        load_stack(sp, b, q, K_RUNS, ks, k_planes)

                def maxima(q):
                    for i in range(3):
                        sp.wait_ge(max_split, 3 * (NQ * b + q) + i + 1)
                        sp.dma_start(qs[ROWS + i:ROWS + i + 1, q % RING, :].rearrange("p (m t) -> p m t", t=P),
                                     mplane[:, i, :]).then_inc(max_in[q % 2], 16)

                for m in range(8):
                    store_planes(m)
                    if m == 0:
                        load(0, keys=False)
                    if m == 4:
                        load(0, queries=False)
                        load(1)
                load(2)
                load(3)
                later = not (isinstance(b, int) and b == 0)
                maxima(0)
                if later:
                    store_tiles(b - 1, (0, 1))
                maxima(1)
                if later:
                    store_tiles(b - 1, (2, 3))
                for q in range(RING, NQ):
                    load(q)
                    maxima(q - 2)
                    if q == 4 and split_x and following is not None:
                        sp.wait_ge(x_split, b + 1)
                        hold(sp, held)
                        at_least(sp, o_read, TT * b)
                        hold(sp, held)
                        at_least(sp, xt_stored, 32 * TT * b)
                        hold(sp, held)
                        load_raw(following)
                    if q == 5 and later:
                        store_rows(b - 1)
                    if q == 6:
                        if not later:
                            sp.wait_ge(w_done, 4)
                        at_least(sp, x_stored, 16 * TT * b)
                        hold(sp, held)
                        at_least(sp, tr_done, TT * b)
                        hold(sp, held)
                        sp.dma_start(y[:, :, :], x_in[b].rearrange("(t p) c -> p t c", p=P)).then_inc(res_in, 16)
                maxima(NQ - 2)
                maxima(NQ - 1)

            body(0, 1)
            with sp.Fori(1, B - 1) as b:
                body(b, b + 1)
            body(B - 1, None)
            store_rows(B - 1)
            store_tiles(B - 1, range(TT))
            if sums_of:
                sp.wait_ge(sums_added, B)
                sp.dma_start(sums_of[1], sums[:, 1, :]).then_inc(sums_stored, 16)
                sp.wait_ge(sums_stored, 16)
            sp.wait_ge(x_stored, 16 * TT * B)
            sp.wait_ge(xt_stored, 32 * TT * B)

        @block.gpsimd
        def _(pool):
            pool.memset(vaug[:, :, :, D:D + 1], 1.0).then_inc(ones_set, 1)
            pool.wait_ge(ones_set, 1)
            pool.memset(ks[ROWS:P, :, :], 1.0).then_inc(ones_set, 1)
            pool.wait_ge(ones_set, 2)
            if sums_of:
                pool.memset(sums[:, 1, :], 0.0).then_inc(ones_set, 1)
                pool.wait_ge(ones_set, 3)

            def load(b):
                for half, dst in zip(xt_in, (x_hi, x_lo)):
                    pool.dma_start(dst[:, :, :], half[b]).then_inc(x_loaded, 16)

            if not split_x:
                load(0)

            def body(b, following):
                for m in range(9):
                    if m < 8:
                        pool.wait_ge(rope_read, 24 * b + 3 * m + 3)
                        pool.tensor_tensor(rope_a(m), rope_a(m), rope_b(m), ALU.add).then_inc(rope_sum, 1)
                    if m >= 1:
                        pool.wait_ge(plane_h, 8 * b + m)
                        pool.tensor_tensor(rope_a(m - 1), rope_a(m - 1), planes(m - 1, 0), ALU.subtract).then_inc(rest_h, 1)
                for h in range(LAST):
                    if h % QUAD == 0 and QUAD <= h <= H:
                        k = h // QUAD - 1
                        pool.wait_ge(maxt_read, NQ * b + k + 1)
                        if k >= 1:
                            pool.wait_ge(max_in[(k - 1) % 2], 48 * (NQ // 2 * b + (k - 1) // 2 + 1))
                        hold(pool, held)
                        pool.tensor_copy(mplane[:, 0, :], mrest[:, :]).then_inc(max_split, 1)
                        pool.wait_ge(max_split, 3 * (NQ * b + k) + 1)
                        pool.tensor_tensor(mrest[:, :], mrest[:, :], mplane[:, 0, :], ALU.subtract).then_inc(max_step, 1)
                        pool.wait_ge(max_step, NQ * b + k + 1)
                        hold(pool, held)
                        pool.tensor_copy(mplane[:, 1, :], mrest[:, :]).then_inc(max_split, 1)
                        pool.wait_ge(max_split, 3 * (NQ * b + k) + 2)
                        pool.tensor_tensor(mplane[:, 2, :], mrest[:, :], mplane[:, 1, :],
                                           ALU.subtract).then_inc(max_split, 1)
                    if sums_of and 2 * QUAD <= h < H and h % QUAD in (1, 2):
                        c = 2 * (h // QUAD - 2) + h % QUAD - 1
                        pool.wait_ge(piece_in[c % SLOTS], 32 * (BESIDE // SLOTS * b + c // SLOTS + 1))
                        pool.tensor_tensor(wpiece[:, c % SLOTS, 0, :], wpiece[:, c % SLOTS, 0, :],
                                           wpiece[:, c % SLOTS, 1, :], ALU.subtract).then_inc(diff_done, 1)
                    if h == (2 if split_x else 3) * QUAD and following is not None:
                        pool.wait_ge(proj_done, 12 * b + 12)
                        hold(pool, held)
                        load(following)
                    if h == 4 * QUAD + 2 and split_x and following is not None:
                        pool.wait_ge(x_loaded, 16 * b + 16)
                        pool.wait_ge(xraw_in, 16 * b + 32)
                        pool.tensor_tensor(flat(x_lo), xraw[:, :], flat(x_hi).bitcast(F32), ALU.subtract).then_inc(x_split, 1)
                        pool.wait_ge(x_split, b + 2)
                    n = h - LAG
                    if n % QUAD == QUAD - 1 and QUAD <= n < H + QUAD:
                        q = n // QUAD - 1
                        pool.wait_ge(rec_done, NQ * b + q + 1)
                        at_least(pool, at_ready, NQ // 2 * b + q // 2)
                        pool.tensor_tensor(un[:, :, q % 2 * D:(q % 2 + 1) * D],
                                           u[:, q % 2, :].rearrange("p (n c) -> p n c", c=32)[:, :, 0:D],
                                           rec[:, q % 2, :].unsqueeze(2).to_broadcast([P, 16, D]),
                                           ALU.mult).then_inc(un_done, 1)
                    if n % 8 == 7 and n >= 15 or n == H + QUAD + 2:
                        g = min(n // 8 - 1, NQ // 2 - 1)
                        if g == 0:
                            at_least(pool, xt_stored, 32 * TT * b)
                        pool.wait_ge(at_hi_done, NQ // 2 * b + g + 1)
                        pool.tensor_tensor(at_lo[:, g, :], at[:, :], at_hi[:, g, :].bitcast(F32),
                                           ALU.subtract).then_inc(at_lo_done, 1)

                if sums_of:
                    pool.wait_ge(abs_done, BESIDE * (b + 1))
                    at_least(pool, sums_added, b)
                    pool.tensor_tensor(sums[:, 1, :], sums[:, 1, :], sums[:, 0, :], ALU.add).then_inc(sums_added, 1)

            body(0, 1)
            with pool.Fori(1, B - 1) as b:
                body(b, b + 1)
            body(B - 1, None)

        @block.scalar
        def _(act):
            if split_x:
                act.wait_ge(xraw_in, 16)
                act.activation(flat(x_hi), xraw[:, :], ACT.Copy).then_inc(x_hi_done, 1)

            def weights_hi(n):
                act.wait_ge(w_loaded[n % 2], 16 * (n // 2 + 1))
                act.activation(flat(w_hi[n]), wraw[:, n % 2, :], ACT.Copy).then_inc(w_hi_done, 1)

            weights_hi(0)
            weights_hi(1)

            def root(b):
                act.wait_ge(root_asked, b + 1)
                act.activation(small[:, 1, :], small[:, 0, :], ACT.Sqrt).then_inc(rooted, 1)

            def copy_tiles(b):
                for t in range(TT):
                    act.wait_ge(tr_done, TT * b + t + 1)
                    act.activation(tiles(0)[:, t, :], tr_bank(t), ACT.Copy).then_inc(tile_hi_done, 1)

            def body(b):
                for m in range(9):
                    if isinstance(b, int) and b == 0 and m == 3:
                        weights_hi(2)
                    if m < 8:
                        act.wait_ge(rope_sum, 8 * b + m + 1)
                        at_least(act, plane_out[m % RR], 32 * b + 16 * (m // RR))
                        act.activation(planes(m, 0), rope_a(m), ACT.Copy).then_inc(plane_h, 1)
                    if m >= 1:
                        act.wait_ge(rest_h, 8 * b + m)
                        act.activation(planes(m - 1, 1), rope_a(m - 1), ACT.Copy).then_inc(plane_m, 1)
                act.wait_ge(ones_set, 2)
                for t in range(TT):
                    if t == TT - 1 and not (isinstance(b, int) and b == 0):
                        root(b - 1)
                    act.wait_ge(proj_done, 12 * b + 9 + t)
                    act.activation(vaug[:, t, :, 0:D], v_bank(t).rearrange("p (h d) -> p h d", d=D),
                                   ACT.Copy).then_inc(v_copied, 1)
                if isinstance(b, int) and b == 0:
                    weights_hi(3)
                else:
                    copy_tiles(b - 1)

                def split_at(g):
                    act.wait_ge(at_ready, NQ // 2 * b + g + 1)
                    act.activation(at_hi[:, g, :], at[:, :], ACT.Copy).then_inc(at_hi_done, 1)

                for i in range(RR):
                    act.wait_ge(plane_out[i], 32 * b + 32)
                def load_piece(c):
                    at_least(act, abs_done, BESIDE * b + max(c - SLOTS + 1, 0))
                    for s in range(2):
                        v = sums_of[0][c * 3 // BESIDE][s].rearrange("p k n -> p (k n)").rearrange("p (c n) -> c p n", n=PIECE)
                        act.dma_start(wpiece[:, c % SLOTS, s, :], v[BESIDE // 3 * b + c % (BESIDE // 3)]).then_inc(
                            piece_in[c % SLOTS], 16)

                def sum_piece(c):
                    act.wait_ge(diff_done, BESIDE * b + c + 1)
                    if c == 0:
                        at_least(act, sums_added, b)
                    act.activation(wpiece[:, c % SLOTS, 0, :], wpiece[:, c % SLOTS, 0, :], ACT.Abs,
                                   accum_out=sums[:, 0, c:c + 1]).then_inc(abs_done, 1)

                if sums_of:
                    load_piece(0)
                    load_piece(1)
                for h in range(H):
                    act.wait_ge(st_done, H * b + h + 1)
                    if h >= PTR:
                        act.wait_ge(pv_done, NQ * b + (h - PTR) // QUAD + 1)
                    act.activation(pt[:, h % PTR, :], ps[1][:, 0:SC], ACT.Exp,
                                   scale=float(D) ** -0.5).then_inc(exp_done, 1)
                    c = 2 * ((h - 3) // QUAD) + (h - 3) % QUAD
                    if sums_of and h >= 3 and (h - 3) % QUAD < 2 and c < BESIDE:
                        if c + 2 < BESIDE:
                            load_piece(c + 2)
                        sum_piece(c)
                    if h % 8 == 6 and h > 8:
                        split_at(h // 8 - 1)
                split_at(NQ // 2 - 1)

            every_b(act, body)
            root(B - 1)
            copy_tiles(B - 1)

        @block.vector
        def _(dve):
            dve.memset(pv[:, :], 0.0).then_inc(consts, 1)

            if split_x:
                dve.wait_ge(x_hi_done, 1)
                dve.tensor_tensor(flat(x_lo), xraw[:, :], flat(x_hi).bitcast(F32), ALU.subtract).then_inc(x_split, 1)

            def weights_lo(n):
                dve.wait_ge(w_hi_done, n + 1)
                dve.tensor_tensor(flat(w_lo[n]), wraw[:, n % 2, :], flat(w_hi[n]).bitcast(F32),
                                  ALU.subtract).then_inc(w_done, 1)

            weights_lo(0)
            weights_lo(1)
            dve.wait_ge(trig_in, 32)

            def more_constants(m):
                if m == 4:
                    weights_lo(2)
                if m == 9:
                    dve.wait_ge(const_in, 32)
                    dve.tensor_copy(identb[:, :], ident[:, :]).then_inc(consts, 1)
                    dve.tensor_copy(flat(masks), at[:, :]).then_inc(consts, 1)
                    dve.wait_ge(consts, 3)

            def norm(b, step):
                st = Steps(dve, norm_steps, b * NORM_STEPS, NORM_STEPS)
                if step == 0:
                    norm_moments(dve, st, y, stats, mv, small, root_asked)
                elif step == 1:
                    st.n = 2 * TT
                    norm_scale(dve, st, small, root_asked, rooted, b)
                else:
                    norm_apply(dve, y, mv, small, normed)

            def split_tile(b, t):
                dve.wait_ge(tile_hi_done, TT * b + t + 1)
                dve.tensor_tensor(tiles(1)[:, t, :], tr_bank(t), tiles(0)[:, t, :].bitcast(F32),
                                  ALU.subtract).then_inc(tile_done, 1)

            def body(b):
                st = Steps(dve, dve_steps, b * DVE_PER, DVE_PER)
                for m in range(10):
                    if isinstance(b, int) and b == 0:
                        more_constants(m)
                    if m < 8:
                        src, c = bank(m % 6), rope_b(m)
                        dve.wait_ge(proj_done, 12 * b + m + 1)
                        at_least(dve, rope_sum, 8 * b + max(m - 1, 0))
                        at_least(dve, plane_l, 8 * b + max(m - RR + 1, 0))
                        dve.tensor_tensor(rope_a(m), src, cosr[:, :], ALU.mult).then_inc(rope_read, 1)
                        dve.tensor_tensor(c[0:64, :], src[64:P, :], sinr[0:64, :], ALU.mult).then_inc(rope_read, 1)
                        dve.tensor_tensor(c[64:P, :], src[0:64, :], sinr[64:P, :], ALU.mult).then_inc(rope_read, 1)
                    if m >= 2:
                        dve.wait_ge(plane_m, 8 * b + m - 1)
                        dve.tensor_tensor(planes(m - 2, 2), rope_a(m - 2), planes(m - 2, 1),
                                          ALU.subtract).then_inc(plane_l, 1)

                def by_token(q):
                    o = q % 2
                    dve.wait_ge(pv_done, NQ * b + q + 1)
                    at_least(dve, un_done, NQ * b + max(q - 1, 0))
                    dve.transpose(u[:, o, :], pv[:, o * NB:(o + 1) * NB]).then_inc(pv_read, 1)
                    dve.wait_ge(pv_read, NQ * b + q + 1)
                    dve.reciprocal(rec[:, o, :], u[:, o, D:T:32]).then_inc(rec_done, 1)

                def by_channel(q):
                    dve.wait_ge(un_done, NQ * b + q + 1)
                    at_least(dve, at_lo_done, NQ // 2 * b + q // 2)
                    dve.transpose(at[:, :], flat(un)).then_inc(at_ready, 1)

                for h in range(LAST):
                    if h < H:
                        if h % QUAD == 0:
                            at_least(dve, qmax_done, NQ * b + h // QUAD)
                        for i, (first, n, c0) in enumerate(((8, 2, 2 * NB), (0, 4, 0), (4, 4, NB))):
                            dve.wait_ge(s_done, 3 * (H * b + h) + i + 1)
                            dve.tensor_reduce(bmax[:, h % QUAD, first:first + n],
                                              ps[0][:, c0:c0 + n * P].rearrange("p (a k) -> p a k", k=P),
                                              AX.X, ALU.max).then_inc(s_read, 1)
                    if h < 3 and not (isinstance(b, int) and b == 0):
                        norm(b - 1, h)
                    q = h // QUAD
                    if h % QUAD == QUAD - 1 and h < H:
                        dve.wait_ge(s_read, 3 * (H * b + h) + 3)
                        at_least(dve, maxt_done, NQ * b + q)
                        for i, (first, n) in enumerate(((7, 1), (8, 2), (4, 3), (0, 4))):
                            if i == 3:
                                st.wait()
                            ins = dve.tensor_reduce(qmax[:, :, i], bmax[:, :, first:first + n], AX.X, ALU.max)
                            if i == 3:
                                ins.then_inc(qmax_done, 1)
                            else:
                                st.inc(ins)
                    if h % QUAD == 0 and QUAD <= h <= H:
                        dve.wait_ge(maxt_done, NQ * b + q)
                        at_least(dve, max_split, 3 * (NQ * b + q - 1))
                        dve.tensor_scalar(mrest[:, :], maxt, -1.0, None, ALU.mult).then_inc(maxt_read, 1)
                    if isinstance(b, int) and b == 0:
                        if h == QUAD:
                            weights_lo(3)
                    else:
                        for t in range(TT):
                            if h == TR_AT[t] + 1:
                                split_tile(b - 1, t)
                    n = h - LAG
                    k = n // QUAD - 1
                    if n % QUAD == QUAD - 1 and 0 <= k < NQ:
                        by_token(k)
                    if n % QUAD == 2 and k % 2 == 0 and 0 < k <= NQ:
                        by_channel(k - 1)
                dve.wait_ge(res_in, 16 * b + 16)
                for t in range(TT):
                    dve.wait_ge(o_done, TT * b + t + 1)
                    dve.tensor_tensor(y[:, t, :], bank(t), y[:, t, :], ALU.add).then_inc(o_read, 1)
                dve.wait_ge(o_read, TT * b + TT)
                st.end()

            every_b(dve, body)
            for step in range(3):
                norm(B - 1, step)
            for t in range(TT):
                split_tile(B - 1, t)

        @block.tensor
        def _(pe):

            def w(n, k, cols):
                return w_hi[n][:, k, cols], w_lo[n][:, k, cols]

            def x(k, cols):
                return x_hi[:, k, cols], x_lo[:, k, cols]

            def transposes(b, t):
                pe.wait_ge(normed, TT * b + TT)
                if not (isinstance(b, int) and b == B - 1):
                    pe.wait_ge(v_copied, TT * b + TT + (4 if t == 2 else 3))
                if t == 3:
                    pe.wait_ge(tile_done, TT * b + 1)
                for k in range(KT):
                    last = pe.transpose(tr_bank(t)[:, k * P:(k + 1) * P], y[:, t, k * P:(k + 1) * P], ident[:, :])
                last.then_inc(tr_done, 1)

            def body(b):
                every = slice(0, T)
                if split_x:
                    pe.wait_ge(x_split, b + 1)
                else:
                    pe.wait_ge(x_loaded, 32 * b + 32)
                for m in range(8):
                    if m < TT:
                        at_least(pe, o_read, TT * b)
                    if m >= 6:
                        pe.wait_ge(rope_read, 24 * b + 3 * (m - 5))
                    if m % 4 == 0:
                        pe.wait_ge(w_done, m // 4 + 1)
                    cols = slice(m % 4 * P, (m % 4 + 1) * P)
                    for k in range(KT):
                        last = product3(pe, bank(m % 6), w(m // 4, k, cols), x(k, every), k == 0, k == KT - 1)
                    last.then_inc(proj_done, 1)

                def project_values(t):
                    if t == 0:
                        pe.wait_ge(w_done, 3)
                    if t < 3:
                        pe.wait_ge(rope_read, 24 * b + 3 * (t + 4))
                    else:
                        pe.wait_ge(v_copied, TT * b + 1)
                    for k in range(KT):
                        last = product3(pe, v_bank(t), x(k, slice(t * P, (t + 1) * P)), w(2, k, every), k == 0, k == KT - 1)
                    last.then_inc(proj_done, 1)

                project_values(0)
                project_values(1)
                pe.wait_ge(rope_read, 24 * b + 24)
                if isinstance(b, int) and b == 0:
                    pe.wait_ge(consts, 3)

                def scores(h):
                    q, c0 = h // QUAD, h % QUAD * T
                    if h % QUAD == 0:
                        pe.wait_ge(stack_in[q % RING], 16 * len(Q_RUNS + K_RUNS) * (NQ // RING * b + q // RING + 1))

                    def one(i, start):
                        return pe.matmul(ps[0][:, S_AT[i]:S_AT[i] + P * (i + 1)],
                                         qs[0:ROWS, q % RING, c0 + i * P:c0 + (i + 1) * P],
                                         ks[0:ROWS, q % RING, c0:c0 + P * (i + 1)],
                                         start=start, stop=False, skip_group_check=True)

                    def mask(a, n):
                        return pe.matmul(ps[0][:, a:a + n], identb[:, :], masks[:, 0, 0:n],
                                         start=False, stop=True, skip_group_check=True)

                    def bank_read(i):
                        if h >= 1:
                            pe.wait_ge(s_read, 3 * (H * b + h - 1) + i + 1)

                    bank_read(0)
                    if h % QUAD == 1 and h > 1:
                        pe.wait_ge(maxt_read, NQ * b + h // QUAD)
                    one(1, True)
                    mask(1152, P).then_inc(s_done, 1)
                    bank_read(1)
                    one(3, True)
                    mask(384, P).then_inc(s_done, 1)
                    bank_read(2)
                    one(2, True)
                    one(0, False)
                    mask(768, 2 * P).then_inc(s_done, 1)

                def scores_t(h):
                    q, c0 = h // QUAD, h % QUAD * T
                    if h % QUAD == 0:
                        pe.wait_ge(max_in[q % 2], 48 * (NQ // 2 * b + q // 2 + 1))
                    at_least(pe, exp_done, H * b + h)
                    if h == 0:
                        pe.wait_ge(v_copied, TT * b + TT)
                        at_least(pe, tile_done, TT * b)
                    rows = ROWS + 3

                    def one(j, start):
                        return pe.matmul(ps[1][:, ST_AT[j]:ST_AT[j] + T - P * j],
                                         ks[0:rows, q % RING, c0 + j * P:c0 + (j + 1) * P],
                                         qs[0:rows, q % RING, c0 + P * j:c0 + T],
                                         start=start, stop=False, skip_group_check=True)

                    def mask(a, n):
                        return pe.matmul(ps[1][:, a:a + n], identb[:, :], masks[:, 1, 0:n],
                                         start=False, stop=True, skip_group_check=True)

                    one(0, True)
                    mask(0, P)
                    one(3, True)
                    one(1, False)
                    mask(512, 2 * P)
                    one(2, True)
                    mask(1024, P).then_inc(st_done, 1)

                def values(q, js):
                    c = q % 2 * NB
                    if js[0] == 0:
                        pe.wait_ge(exp_done, H * b + QUAD * (q + 1))
                        if q >= 2:
                            pe.wait_ge(pv_read, NQ * b + q - 1)
                    for j in js:
                        for g in range(QUAD):
                            h = QUAD * q + g
                            last = pe.matmul(pv[32 * g:32 * g + D + 1, c + j * P:c + T], vaug[:, j, h, :],
                                             pt[:, h % PTR, ST_AT[j]:ST_AT[j] + T - P * j],
                                             start=j == 0, stop=j == TT - 1)
                    if js[-1] == TT - 1:
                        last.then_inc(pv_done, 1)

                def project_out(groups, tiles):
                    if groups[0] == 0:
                        pe.wait_ge(w_done, 4)
                        pe.wait_ge(s_read, 3 * H * (b + 1))
                        pe.wait_ge(maxt_read, NQ * (b + 1))
                    if TT - 1 in tiles:
                        pe.wait_ge(exp_done, H * (b + 1))
                    for g in groups:
                        pe.wait_ge(at_lo_done, NQ // 2 * b + g + 1)
                        for t in tiles:
                            cols = slice(t * P, (t + 1) * P)
                            last = product3(pe, bank(t), (at_hi[:, g, cols], at_lo[:, g, cols]), w(3, g, every),
                                            g == 0, g == NQ // 2 - 1)
                            if g == NQ // 2 - 1:
                                last.then_inc(o_done, 1)

                for h in range(LAST):
                    if h < H:
                        scores(h)
                    if h < 2:
                        project_values(h + 2)
                    if h in TR_AT and not (isinstance(b, int) and b == 0):
                        for t in range(TT):
                            if h == TR_AT[t]:
                                transposes(b - 1, t)
                    n = h - LAG
                    if 0 <= n < H:
                        scores_t(n)
                    if h % QUAD == 0 and QUAD <= h <= H:
                        pe.wait_ge(qmax_done, NQ * b + h // QUAD)
                        pe.wait_ge(s_read, 3 * (H * b + min(h, H - 1)) + 1)
                        pe.transpose(maxt, qmax[:, :, :].rearrange("p h i -> p (h i)"), ident[:, :]).then_inc(maxt_done, 1)
                    if H < h <= H + 2:
                        project_out((h - H - 1,), range(3))
                    if QUAD <= n < H + QUAD and n % QUAD < 3:
                        values(n // QUAD - 1, ((0,), (1,), (2, 3))[n % QUAD])
                project_out(range(2), range(3, TT))
                project_out(range(2, NQ // 2), range(TT))

            every_b(pe, body)
            for t in range(TT):
                transposes(B - 1, t)


GT = 2
GROUPS = FT // GT


def gated_ffn_phase(nc, tag, x_in, xt_in, pairs, sums_in, ident_in, x_out, xt_out, nf4_in, nf4_out):
    HALF = P // 2
    with ExitStack() as ctx:
        def sb(name, shape, dt=F32, at=ctx):
            return at.enter_context(nc.sbuf_tensor(f"{tag}_{name}", shape, dt))

        def sem(name):
            return nc.alloc_semaphore(f"{tag}_{name}")

        with ExitStack() as early:
            wd = [sb(f"w{n}_diff", s, at=early) for n, s in enumerate(([P, KT, F], [P, KT, F], [P, FT, C]))]
            wb = [sb(f"w{n}_base", s, at=early) for n, s in enumerate(([P, KT, F], [P, KT, F], [P, FT, C]))]
        w_hi = [sb(f"w{n}_hi", s, F32R) for n, s in enumerate(([P, KT, F], [P, KT, F], [P, FT, C]))]
        w_lo = [sb(f"w{n}_lo", s, F32R) for n, s in enumerate(([P, KT, F], [P, KT, F], [P, FT, C]))]
        x_hi = sb("x_hi", [P, KT, T], F32R)
        x_lo = sb("x_lo", [P, KT, T], F32R)
        with ExitStack() as early:
            made = sb("made", [P, 2, GT * C], at=early)
        y = sb("y", [P, TT, T])
        gate = sb("gate", [P, 2, T])
        h_hi = sb("h_hi", [P, 2, T], F32R)
        h_lo = sb("h_lo", [P, 2, T], F32R)
        sums = sb("sums", [P, 3, BESIDE // 3])
        total = sb("total", [P, 3])
        coeff = sb("coeff", [P, 3])
        ident = sb("ident", [P, P])
        stats = sb("stats", [P, TT, 6])
        mv = sb("mv", [P, TT, 2])
        small = sb("small", [P, 4, TT])
        idx = sb("idx", [P, P], I32)
        scale = sb("scale", [P, P])
        code = sb("code", [P, 2, P])
        nw = sb("nw", [P, P])
        nw_hi = sb("nw_hi", [P, P], F32R)
        ps = ctx.enter_context(nc.psum_tensor(f"{tag}_ps", [P, 8, NB], F32))

        raw_in = [sem(f"raw_in{g}") for g in range(GROUPS + 2)]
        diff_done, ones_set, ident_set, sums_set = sem("diff_done"), sem("ones_set"), sem("ident_set"), sem("sums_in")
        sum_done, total_done, coeff_done = sem("sum_done"), sem("total_done"), sem("coeff_done")
        sign_done, w_made, w_hi_done, w_done = sem("sign_done"), sem("w_made"), sem("w_hi_done"), sem("w_done")
        x_loaded = sem("x_loaded")
        up_done, silu_done, h_done, h_hi_done, h_lo_done, down_done = (
            sem("up_done"), sem("silu_done"), sem("h_done"), sem("h_hi_done"), sem("h_lo_done"), sem("down_done"))
        res_in, o_read = sem("res_in"), sem("o_read")
        root_asked, rooted, normed = sem("root_asked"), sem("rooted"), sem("normed")
        tr_done, tile_hi_done, tile_done, x_stored = sem("tr_done"), sem("tile_hi_done"), sem("tile_done"), sem("x_stored")
        xt_stored = [sem("xt_stored0"), sem("xt_stored1")]
        piece_in, nf4_step, nf4_stored = sem("piece_in"), sem("nf4_step"), sem("nf4_stored")
        held = sem("held")
        dve_steps = sem("dve_steps")
        block = ctx.enter_context(nc.Block())
        N = 3 * GROUPS

        def part(tensors, i):
            g, n = i // 3, i % 3
            if n == 2:
                return tensors[2][:, g * GT:(g + 1) * GT, :]
            return tensors[n][:, :, g * GT * P:(g + 1) * GT * P]

        def in_part(ap, i):
            return ap.rearrange("p (k n) -> p k n", k=GT if i % 3 == 2 else KT)

        def tile(half, t):
            return y[:, 2 * (t % 2) + half, :]

        def every_b(eng, body):
            body(0)
            with eng.Fori(1, B) as b:
                body(b)

        def first(b):
            return isinstance(b, int) and b == 0

        @block.sync
        def _(sp):
            sp.dma_start(flat(sums), sums_in).then_inc(sums_set, 16)
            sp.dma_start(ident[:, :], ident_in).then_inc(ident_set, 16)
            for i in range(N):
                if i == 3:
                    sp.wait_ge(x_loaded, 32)
                for s, dst in enumerate((wd, wb)):
                    sp.dma_start(part(dst, i), part([p[s] for p in pairs], i)).then_inc(raw_in[i if i < 3 else i // 3 + 2], 16)

            def store_rows(b):
                for t in range(TT):
                    sp.wait_ge(normed, TT * b + t + 1)
                    sp.dma_start(x_out[b, t * P:(t + 1) * P, :], y[:, t, :]).then_inc(x_stored, 16)

            def store_tiles(b):
                for t in range(TT):
                    sp.wait_ge(tile_done, TT * b + t + 1)
                    for half in range(2):
                        sp.dma_start(xt_out[half][b, :, :, t * P:(t + 1) * P],
                                     tile(half, t).rearrange("p (k t) -> p k t", k=KT)).then_inc(xt_stored[t % 2], 16)

            def body(b):
                if first(b):
                    sp.wait_ge(w_done, N)
                else:
                    store_tiles(b - 1)
                    sp.wait_ge(xt_stored[0], 64 * b)
                    hold(sp, held)
                    sp.wait_ge(xt_stored[1], 64 * b)
                    hold(sp, held)
                sp.dma_start(y[:, :, :], x_in[b].rearrange("(t p) c -> p t c", p=P)).then_inc(res_in, 16)
                store_rows(b)

            every_b(sp, body)
            store_tiles(B - 1)
            sp.wait_ge(x_stored, 16 * TT * B)
            sp.wait_ge(xt_stored[0], 64 * B)
            sp.wait_ge(xt_stored[1], 64 * B)

        @block.gpsimd
        def _(pool):
            i_parts = nf4_in[0].rearrange("p k (g n) -> (k g) p n", n=P)
            s_parts = nf4_in[1].rearrange("h k (g n) -> (k g) h n", n=P)
            o_parts = [o.rearrange("p k (g n) -> (k g) p n", n=P) for o in nf4_out]
            STEPS = 2 * len(NF4) + 2
            PIECES = KT * C // P // B

            def load(b):
                for half, dst in enumerate((x_hi, x_lo)):
                    pool.dma_start(dst[:, :, :], xt_in[half][b]).then_inc(x_loaded, 16)

            def piece(c):
                st = Steps(pool, nf4_step, c * STEPS, STEPS)
                at_least(pool, nf4_step, STEPS * c)
                hold(pool, held)
                pool.dma_start(idx[:, :], i_parts[c]).then_inc(piece_in, 16)
                for half in range(2):
                    pool.dma_start(scale[half * HALF:(half + 1) * HALF, :],
                                   s_parts[c, half:half + 1].to_broadcast([HALF, P])).then_inc(piece_in, 16)
                pool.wait_ge(piece_in, 48 * c + 48)
                at_least(pool, nf4_stored, 32 * c)
                hold(pool, held)
                st.inc(pool.tensor_scalar(nw[:, :], idx[:, :], 0.0, NF4[0], ALU.is_equal, ALU.mult))
                for n, value in enumerate(NF4):
                    if n:
                        st.inc(pool.tensor_scalar(code[:, n % 2, :], idx[:, :], float(n), value, ALU.is_equal, ALU.mult))
                        st.wait()
                        st.inc(pool.tensor_tensor(nw[:, :], nw[:, :], code[:, n % 2, :], ALU.add))
                st.wait()
                st.done(pool.tensor_tensor(nw[:, :], nw[:, :], scale[:, :], ALU.mult))
                hold(pool, held)
                st.done(pool.tensor_copy(nw_hi[:, :], nw[:, :]))
                st.done(pool.tensor_tensor(code[:, 0, :], nw[:, :], nw_hi[:, :].bitcast(F32), ALU.subtract))
                st.end()
                hold(pool, held)
                pool.dma_start(o_parts[0][c], nw_hi[:, :].bitcast(F32)).then_inc(nf4_stored, 16)
                pool.dma_start(o_parts[1][c], code[:, 0, :]).then_inc(nf4_stored, 16)

            def body(b, following):
                for c in range(0 if first(b) else -1, PIECES - (following is not None)):
                    piece(PIECES * b + c)
                if following is not None:
                    pool.wait_ge(up_done, 2 * FT * (b + 1))
                    hold(pool, held)
                    load(following)

            load(0)
            body(0, 1)
            with pool.Fori(1, B - 1) as b:
                body(b, b + 1)
            body(B - 1, None)
            pool.wait_ge(nf4_stored, 32 * KT * C // P)

        @block.scalar
        def _(act):
            def make(start, end):
                for i in range(start, end):
                    act.wait_ge(diff_done, i + 1)
                    act.activation(part(wd, i), part(wd, i), ACT.Sign).then_inc(sign_done, 1)
                for i in range(start, end):
                    act.wait_ge(w_made, i + 1)
                    act.activation(part(w_hi, i), in_part(made[:, i % 2, :], i), ACT.Copy).then_inc(w_hi_done, 1)

            def copy_tiles(b):
                for t in range(TT):
                    act.wait_ge(tr_done, TT * b + TT)
                    if t < 2:
                        act.wait_ge(x_stored, 16 * TT * (b + 1))
                    at_least(act, xt_stored[t % 2], 64 * b + 32 * (t // 2))
                    act.activation(tile(0, t).bitcast(F32R), ps[:, t, :], ACT.Copy).then_inc(tile_hi_done, 1)

            make(0, 2)
            make(2, 3)
            make(3, 6)

            def body(b):
                for f in range(FT):
                    n = FT * b + f
                    act.wait_ge(up_done, 2 * n + 1)
                    at_least(act, h_lo_done, max(f - 1, 0) + FT * b)
                    act.activation(gate[:, f % 2, :], ps[:, 4 + f % 2 * 2, :], ACT.Silu).then_inc(silu_done, 1)
                    act.wait_ge(h_done, n + 1)
                    at_least(act, down_done, FT * b + max(f - 1, 0))
                    act.activation(h_hi[:, f % 2, :], gate[:, f % 2, :], ACT.Copy).then_inc(h_hi_done, 1)
                    if f == 1 and not first(b):
                        copy_tiles(b - 1)
                    if first(b) and f % 2 == 0 and f // 2 + 2 < GROUPS:
                        make(3 * (f // 2 + 2), 3 * (f // 2 + 3))
                act.wait_ge(root_asked, b + 1)
                act.activation(small[:, 1, :], small[:, 0, :], ACT.Sqrt).then_inc(rooted, 1)

            every_b(act, body)
            copy_tiles(B - 1)

        DVE_PER = NORM_STEPS

        @block.vector
        def _(dve):
            dve.memset(y[:, 0, 0:P], 1.0).then_inc(ones_set, 1)
            dve.wait_ge(sums_set, 16)
            dve.tensor_reduce(total[:, :], sums[:, :, :], AX.X, ALU.add).then_inc(sum_done, 1)
            dve.wait_ge(total_done, 1)
            dve.tensor_scalar(coeff[:, :], ps[:, 4, 0:3], 1.0 / (C * F), None, ALU.mult).then_inc(coeff_done, 1)
            dve.wait_ge(coeff_done, 1)

            def make(start, end):
                for i in range(start, end):
                    dve.wait_ge(raw_in[i if i < 3 else i // 3 + 2], 32 if i < 3 else 96)
                    dve.tensor_tensor(part(wd, i), part(wd, i), part(wb, i), ALU.subtract).then_inc(diff_done, 1)
                for i in range(start, end + 1):
                    if i < end:
                        dve.wait_ge(sign_done, i + 1)
                        if i >= 2:
                            dve.wait_ge(w_done, i - 1)
                        dve.scalar_tensor_tensor(out=in_part(made[:, i % 2, :], i), in0=part(wd, i),
                                                 scalar=coeff[:, i % 3:i % 3 + 1], in1=part(wb, i),
                                                 op0=ALU.mult, op1=ALU.add).then_inc(w_made, 1)
                    if i > start:
                        j = i - 1
                        dve.wait_ge(w_hi_done, j + 1)
                        dve.tensor_tensor(part(w_lo, j), in_part(made[:, j % 2, :], j), part(w_hi, j).bitcast(F32),
                                          ALU.subtract).then_inc(w_done, 1)

            make(0, 2)
            make(2, 3)
            make(3, 6)

            def split_tiles(b):
                for t in range(TT):
                    dve.wait_ge(tile_hi_done, TT * b + t + 1)
                    dve.tensor_tensor(tile(1, t), ps[:, t, :], tile(0, t), ALU.subtract).then_inc(tile_done, 1)

            def body(b):
                st = Steps(dve, dve_steps, b * DVE_PER, DVE_PER)
                for f in range(FT):
                    n = FT * b + f
                    dve.wait_ge(silu_done, n + 1)
                    dve.wait_ge(up_done, 2 * n + 2)
                    dve.tensor_tensor(gate[:, f % 2, :], ps[:, 5 + f % 2 * 2, :], gate[:, f % 2, :], ALU.mult).then_inc(h_done, 1)
                    dve.wait_ge(h_hi_done, n + 1)
                    dve.tensor_tensor(h_lo[:, f % 2, :], gate[:, f % 2, :], h_hi[:, f % 2, :].bitcast(F32),
                                      ALU.subtract).then_inc(h_lo_done, 1)
                    if f == 1 and not first(b):
                        split_tiles(b - 1)
                    if first(b) and f % 2 == 0 and f // 2 + 2 < GROUPS:
                        make(3 * (f // 2 + 2), 3 * (f // 2 + 3))
                dve.wait_ge(res_in, 16 * b + 16)
                dve.wait_ge(down_done, FT * (b + 1))
                for t in range(TT):
                    dve.tensor_tensor(y[:, t, :], ps[:, t, :], y[:, t, :], ALU.add).then_inc(o_read, 1)
                    dve.wait_ge(o_read, TT * b + t + 1)
                norm_rows(dve, st, y, stats, mv, small, root_asked, rooted, normed, b)

            every_b(dve, body)
            split_tiles(B - 1)

        @block.tensor
        def _(pe):
            pe.wait_ge(ones_set, 1)
            pe.wait_ge(sum_done, 1)
            pe.matmul(ps[:, 4, 0:3], y[:, 0, 0:P], total[:, :], start=True, stop=True).then_inc(total_done, 1)
            pe.wait_ge(coeff_done, 1)
            pe.wait_ge(ident_set, 16)

            def transposes(b):
                for t in range(TT):
                    pe.wait_ge(normed, TT * b + t + 1)
                    for k in range(KT):
                        last = pe.transpose(ps[:, t, k * P:(k + 1) * P], y[:, t, k * P:(k + 1) * P], ident[:, :])
                    last.then_inc(tr_done, 1)

            def body(b):
                def up(f):
                    if first(b):
                        pe.wait_ge(w_done, 3 * (f // GT) + 2)
                    if f >= 2:
                        pe.wait_ge(h_done, FT * b + f - 1)
                    else:
                        at_least(pe, h_done, FT * b)
                    cols = slice(f * P, (f + 1) * P)
                    for m in range(2):
                        for k in range(KT):
                            last = product3(pe, ps[:, 4 + f % 2 * 2 + m, :], (w_hi[m][:, k, cols], w_lo[m][:, k, cols]),
                                            (x_hi[:, k, :], x_lo[:, k, :]), k == 0, k == KT - 1)
                        last.then_inc(up_done, 1)

                def down(f):
                    if first(b):
                        pe.wait_ge(w_done, 3 * (f // GT) + 3)
                    pe.wait_ge(h_lo_done, FT * b + f + 1)
                    for t in range(TT):
                        cols = slice(t * P, (t + 1) * P)
                        last = product3(pe, ps[:, t, :], (h_hi[:, f % 2, cols], h_lo[:, f % 2, cols]),
                                        (w_hi[2][:, f, :], w_lo[2][:, f, :]), f == 0, f == FT - 1)
                    last.then_inc(down_done, 1)

                pe.wait_ge(x_loaded, 32 * b + 32)
                up(0)
                up(1)
                if not first(b):
                    transposes(b - 1)
                for f in range(2, FT):
                    up(f)
                    if f == 2:
                        at_least(pe, tile_done, TT * b)
                    down(f - 2)
                down(FT - 2)
                down(FT - 1)

            every_b(pe, body)
            transposes(B - 1)


def quantised_ffn_phase(nc, tag, x_in, xt_in, w_in_halves, bias, out):
    with ExitStack() as ctx:
        def sb(name, shape, dt=F32):
            return ctx.enter_context(nc.sbuf_tensor(f"{tag}_{name}", shape, dt))

        def sem(name):
            return nc.alloc_semaphore(f"{tag}_{name}")

        w_hi = sb("w_hi", [P, KT, C], F32R)
        w_lo = sb("w_lo", [P, KT, C], F32R)
        biasr = sb("biasr", [P, C])
        x_hi = sb("x_hi", [P, 2, KT, T], F32R)
        x_lo = sb("x_lo", [P, 2, KT, T], F32R)
        y = sb("y", [P, 2, TT, T])
        stats = sb("stats", [P, TT, 6])
        mv = sb("mv", [P, TT, 2])
        small = sb("small", [P, 4, TT])
        ps = ctx.enter_context(nc.psum_tensor(f"{tag}_ps", [P, 8, NB], F32))

        w_loaded, bias_in, x_loaded = sem("w_loaded"), sem("bias_in"), [sem("x_loaded0"), sem("x_loaded1")]
        res_in, biased, o_done, o_read = [sem("res_in0"), sem("res_in1")], sem("biased"), sem("o_done"), sem("o_read")
        root_asked, rooted, normed = sem("root_asked"), sem("rooted"), sem("normed")
        stored, dve_steps = [sem("stored0"), sem("stored1")], sem("dve_steps")
        block = ctx.enter_context(nc.Block())

        @block.sync
        def _(sp):
            for b in range(B):
                i = b % 2
                if b == 0:
                    sp.wait_ge(x_loaded[0], 32)
                    sp.dma_start(biasr[:, :], bias.to_broadcast([P, C])).then_inc(bias_in, 16)
                if b >= 2:
                    sp.wait_ge(stored[i], 16 * TT * (b // 2))
                sp.dma_start(y[:, i, :, :], x_in[b].rearrange("(t p) c -> p t c", p=P)).then_inc(res_in[i], 16)

        @block.gpsimd
        def _(pool):
            for half, dst in enumerate((w_hi, w_lo)):
                pool.dma_start(dst[:, :, :], w_in_halves[half]).then_inc(w_loaded, 16)

            def load(b):
                if b >= 2:
                    pool.wait_ge(o_done, TT * (b - 1))
                for half, dst in enumerate((x_hi, x_lo)):
                    pool.dma_start(dst[:, b % 2, :, :], xt_in[half][b]).then_inc(x_loaded[b % 2], 16)

            load(0)
            for b in range(B):
                if b + 1 < B:
                    load(b + 1)
                pool.wait_ge(bias_in, 16)
                pool.wait_ge(res_in[b % 2], 16 * (b // 2 + 1))
                for t in range(TT):
                    pool.tensor_tensor(y[:, b % 2, t, :], y[:, b % 2, t, :], biasr[:, :], ALU.add).then_inc(biased, 1)

        @block.scalar
        def _(act):
            for b in range(B):
                act.wait_ge(root_asked, b + 1)
                act.activation(small[:, 1, :], small[:, 0, :], ACT.Sqrt).then_inc(rooted, 1)
                for t in range(TT):
                    act.wait_ge(normed, TT * b + t + 1)
                    act.dma_start(out[b, t * P:(t + 1) * P, :], y[:, b % 2, t, :]).then_inc(stored[b % 2], 16)
            act.wait_ge(stored[0], 16 * TT * B // 2)
            act.wait_ge(stored[1], 16 * TT * B // 2)

        @block.vector
        def _(dve):
            for b in range(B):
                st = Steps(dve, dve_steps, b * NORM_STEPS, NORM_STEPS)
                dve.wait_ge(biased, TT * (b + 1))
                for t in range(TT):
                    dve.wait_ge(o_done, TT * b + t + 1)
                    dve.tensor_tensor(y[:, b % 2, t, :], ps[:, b % 2 * TT + t, :], y[:, b % 2, t, :], ALU.add).then_inc(o_read, 1)
                    dve.wait_ge(o_read, TT * b + t + 1)
                norm_rows(dve, st, y[:, b % 2, :, :], stats, mv, small, root_asked, rooted, normed, b)
                st.end()

        @block.tensor
        def _(pe):
            pe.wait_ge(w_loaded, 32)
            for b in range(B):
                pe.wait_ge(x_loaded[b % 2], 32 * (b // 2 + 1))
                if b >= 2:
                    pe.wait_ge(o_read, TT * (b - 1))
                for t in range(TT):
                    cols = slice(t * P, (t + 1) * P)
                    for k in range(KT):
                        last = product3(pe, ps[:, b % 2 * TT + t, :], (x_hi[:, b % 2, k, cols], x_lo[:, b % 2, k, cols]),
                                        (w_hi[:, k, :], w_lo[:, k, :]), k == 0, k == KT - 1)
                    last.then_inc(o_done, 1)


def head_channels(order):
    rows = []
    for tile in range(C // P):
        for d in range(D):
            half, i = d // (D // 2), d % (D // 2)
            within = 2 * i + half if order == "pairs" else half * (D // 2) + i
            rows += [(tile * 2 * QUAD + h) * D + within for h in range(2 * QUAD)]
    return np.array(rows)


def output_channels():
    return np.array([((2 * g + o) * QUAD + h) * D + d
                     for g in range(NQ // 2) for h in range(QUAD) for o in range(2) for d in range(D)])


def rotary(order):
    f = np.float32
    t = np.arange(T, dtype=f)
    if order == "pairs":
        freqs = np.ones(D // 2, f)
    else:
        freqs = (f(1.0) / np.power(f(10000.0), np.arange(0, D, 2, dtype=f) / f(D))).astype(f)
    theta = (t[None, :] * freqs[:, None]).astype(f).astype(np.float64)
    cos = np.repeat(np.concatenate([np.cos(theta)] * 2), 2 * QUAD, axis=0).astype(f)
    sin = np.repeat(np.concatenate([-np.sin(theta), np.sin(theta)]), 2 * QUAD, axis=0).astype(f)
    return cos, sin


def by_partition(w):
    k, n = w.shape
    return np.ascontiguousarray(w.reshape(k // P, P, n).transpose(1, 0, 2))


def causal_masks():
    later = np.triu(np.ones((P, P)), 1) * -1e30
    return np.concatenate([later, later, later.T, later.T], axis=1).astype(np.float32)


def two_layers(nc, x, xt, l0, ffn, l1, rope0, rope1, ident, masks, w_idx, absmax, bias, out):
    def rows(name):
        return nc.dram_tensor(name, [B, T, C], F32).ap()

    def channels(name):
        return nc.dram_tensor(name, [B, P, KT, T], F32).ap()

    q_planes = nc.dram_tensor("q_planes", [B, C // P, 3, P, T], BF16).ap()
    k_planes = nc.dram_tensor("k_planes", [B, C // P, 3, P, T], BF16).ap()
    def halves(name):
        return [channels(f"{name}_hi"), channels(f"{name}_lo")]

    x1, x2, x3 = rows("x1"), rows("x2"), rows("x3")
    x1t, x2t, x3t = halves("x1t"), halves("x2t"), halves("x3t")
    sums = nc.dram_tensor("sums", [P, BESIDE], F32).ap()
    nf4 = [nc.dram_tensor(f"nf4_{half}", [P, KT, C], F32).ap() for half in ("hi", "lo")]
    with nc.cleanup_on_exit():
        attention_phase(nc, "a0", x, [xt], l0, *rope0, ident, masks, x1, x1t, q_planes, k_planes, (ffn, sums))
    with nc.cleanup_on_exit():
        gated_ffn_phase(nc, "f0", x1, x1t, ffn, sums, ident, x2, x2t, (w_idx, absmax), nf4)
    with nc.cleanup_on_exit():
        attention_phase(nc, "a1", x2, x2t, l1, *rope1, ident, masks, x3, x3t, q_planes, k_planes)
    with nc.cleanup_on_exit():
        quantised_ffn_phase(nc, "f1", x3, x3t, nf4, bias, out)


def kernel(**inputs):
    import concourse.bacc as bacc
    from concourse.bass_utils import run_bass_kernel_spmd

    g = {n: np.asarray(a) for n, a in inputs.items()}
    x = g["L0_attn_x"]
    arrays = {
        "x": x,
        "xt": np.ascontiguousarray(x.transpose(0, 2, 1).reshape(B, KT, P, T).transpose(0, 2, 1, 3)),
    }
    for layer, order in ((0, "pairs"), (1, "halves")):
        ch = head_channels(order)
        for n in "qk":
            arrays[f"w{n}{layer}"] = by_partition(g[f"L{layer}_attn_w{n}"][ch].T)
        arrays[f"wv{layer}"] = by_partition(g[f"L{layer}_attn_wv"].T)
        arrays[f"wo{layer}"] = by_partition(g[f"L{layer}_attn_wo"].T[output_channels()])
        arrays[f"cos{layer}"], arrays[f"sin{layer}"] = rotary(order)
    for n in (1, 3, 2):
        arrays[f"w{n}"] = by_partition(g[f"L0_ffn_w{n}"].T)
        arrays[f"mean_w{n}"] = by_partition(g[f"L0_ffn_mean_w{n}"].T)
    arrays["ident"] = np.eye(P, dtype=np.float32)
    arrays["masks"] = causal_masks()
    arrays["w_idx"] = by_partition(g["L1_ffn_w_idx"].T)
    arrays["absmax"] = np.ascontiguousarray(g["L1_ffn_absmax"].reshape(C, KT, 2).transpose(2, 1, 0))
    arrays["bias"] = g["L1_ffn_bias"].reshape(1, C)

    nc = bacc.Bacc("TRN2", target_bir_lowering=False, num_devices=1)
    arrays = {f"in_{n}": np.ascontiguousarray(a) for n, a in arrays.items()}
    t = {n[3:]: nc.dram_tensor(n, a.shape, mybir.dt.from_np(a.dtype), kind="ExternalInput").ap()
         for n, a in arrays.items()}
    out = nc.dram_tensor("out", (B, T, C), F32, kind="ExternalOutput").ap()
    two_layers(nc, t["x"], t["xt"], [t[f"w{n}0"] for n in "qkvo"],
               [(t[f"w{n}"], t[f"mean_w{n}"]) for n in (1, 3, 2)], [t[f"w{n}1"] for n in "qkvo"],
               (t["cos0"], t["sin0"]), (t["cos1"], t["sin1"]), t["ident"], t["masks"],
               t["w_idx"], t["absmax"], t["bias"], out)
    r = run_bass_kernel_spmd(nc, [arrays], core_ids=[0])
    return r.results[0]["out"]
```
